# Optimizing a Trainium2 kernel written in Bass

```python
import numpy as np
import jax
import jax.numpy as jnp

def _softmax(x, axis=-1):
    return jax.nn.softmax(x, axis=axis)

def _gelu(x):
    return jax.nn.gelu(x, approximate=True)

def _silu(x):
    return jax.nn.silu(x)

def _sigmoid(x):
    return jax.nn.sigmoid(x)

def _layernorm(x, axis=-1, eps=1e-05):
    m = jnp.mean(x, axis=axis, keepdims=True)
    v = jnp.var(x, axis=axis, keepdims=True)
    return (x - m) / jnp.sqrt(v + eps)

def _scatter_add(tgt, idx, src, axis=0):
    return tgt.at[idx].add(src)

def _segment_sum(src, seg, n):
    return jax.ops.segment_sum(src, seg, n)
kernel_name = 'mk_gnn_preln_d4_gnn_r32_5a32ae'

def setup_inputs(seed: int=0):
    np.random.seed(seed)
    _w = jnp.asarray

    def _rec_inputs():
        import jax
        import jax.numpy as jnp
        _gk = jax.random.key(seed)
        x = -0.0002117 + 1 * jax.random.normal(jax.random.fold_in(_gk, 1), (3125, 256), jnp.float32)
        src = jax.random.randint(jax.random.fold_in(_gk, 2), (50000,), 0, 3125, jnp.int32)
        dst = jax.random.randint(jax.random.fold_in(_gk, 3), (50000,), 0, 3125, jnp.int32)
        _o = jnp.argsort(dst, stable=True)
        src = src[_o]
        dst = dst[_o]
        edge_attr_64 = -5.3897e-05 + 0.999841 * jax.random.normal(jax.random.fold_in(_gk, 12), (50000, 64), jnp.float32)
        edge_weight = jax.random.uniform(jax.random.fold_in(_gk, 14), (50000,), jnp.float32, 0.0, 1)
        return (x, src, dst, edge_attr_64, edge_weight)
    x, src, dst, edge_attr_64, edge_weight = _rec_inputs()

    def _L0_gnn_setup():
        import jax, jax.numpy as jnp
        import numpy as np
        N_NODES = 3125
        N_EDGES = 100000
        D_IN = 256
        D_HID = 256
        D_OUT = 256

        def _sage_conv(x, src, tgt, W_l, b_l, W_r):
            n = x.shape[0]
            msgs = x[src]
            agg = jax.ops.segment_sum(msgs, tgt, num_segments=n)
            deg = jax.ops.segment_sum(jnp.ones((src.shape[0],), x.dtype), tgt, num_segments=n)
            agg = agg / jnp.maximum(deg, 1.0)[:, None]
            return agg @ W_l + b_l + x @ W_r
        key = jax.random.key(seed)
        ks = jax.random.split(key, 8)
        x = jax.random.normal(ks[0], (N_NODES, D_IN), dtype=jnp.float32)
        edge_index = jax.random.randint(ks[1], (2, N_EDGES), 0, N_NODES, dtype=jnp.int64)
        s1 = 1.0 / np.sqrt(D_IN)
        s2 = 1.0 / np.sqrt(D_HID)
        return {'x': x, 'edge_index': edge_index, 'W_l1': jax.random.uniform(ks[2], (D_IN, D_HID), jnp.float32, -s1, s1), 'b1': jnp.zeros((D_HID,), jnp.float32), 'W_r1': jax.random.uniform(ks[3], (D_IN, D_HID), jnp.float32, -s1, s1), 'W_l2': jax.random.uniform(ks[4], (D_HID, D_OUT), jnp.float32, -s2, s2), 'b2': jnp.zeros((D_OUT,), jnp.float32), 'W_r2': jax.random.uniform(ks[5], (D_HID, D_OUT), jnp.float32, -s2, s2)}
    _L0_gnn_all = _L0_gnn_setup()
    _L0_gnn_in = {k: v for k, v in _L0_gnn_all.items() if k in ('W_l1', 'b1', 'W_r1', 'W_l2', 'b2', 'W_r2')}
    del _L0_gnn_all

    def _L1_gnn_setup():
        import jax, jax.numpy as jnp
        import numpy as np
        N_NODES = 3125
        N_EDGES = 100000
        D_IN = 256
        D_OUT = 256
        key = jax.random.key(seed)
        k1, k2, k3, k4, k5, k6 = jax.random.split(key, 6)
        x = jax.random.normal(k1, (N_NODES, D_IN), dtype=jnp.float32)
        edge_val = jax.random.uniform(k2, (N_EDGES,), dtype=jnp.float32)
        stdv = 1.0 / np.sqrt(D_OUT)
        W = jax.random.uniform(k3, (D_IN, D_OUT), dtype=jnp.float32, minval=-stdv, maxval=stdv)
        b = jax.random.uniform(k4, (D_OUT,), dtype=jnp.float32, minval=-stdv, maxval=stdv)
        edge_row = jax.random.randint(k5, (N_EDGES,), 0, N_NODES, dtype=jnp.int32)
        edge_col = jax.random.randint(k6, (N_EDGES,), 0, N_NODES, dtype=jnp.int32)
        return {'x': x, 'edge_val': edge_val, 'W': W, 'b': b, 'edge_row': edge_row, 'edge_col': edge_col}
    _L1_gnn_all = _L1_gnn_setup()
    _L1_gnn_in = {k: v for k, v in _L1_gnn_all.items() if k in ('W', 'b')}
    del _L1_gnn_all

    def _L2_gnn_setup():
        import jax, jax.numpy as jnp
        import numpy as np
        N_NODES = 50000
        N_EDGES = 12500
        D_NODE = 256
        D_EDGE = 64
        LN_EPS = 1e-06

        def _layer_norm(x, scale, bias):
            mu = jnp.mean(x, axis=-1, keepdims=True)
            var = jnp.mean(jnp.square(x - mu), axis=-1, keepdims=True)
            return (x - mu) * jax.lax.rsqrt(var + LN_EPS) * scale + bias

        def _glorot(key, shape):
            fan_in, fan_out = shape
            std = jnp.sqrt(2.0 / (fan_in + fan_out))
            return std * jax.random.normal(key, shape, dtype=jnp.float32)

        def _relu_mlp_skip(x, Ws, bs):
            n = len(Ws)
            for i, (W, b) in enumerate(zip(Ws, bs)):
                y = x @ W + b
                if i < n - 1:
                    y = jax.nn.relu(y)
                x = x + y if y.shape[-1] == x.shape[-1] else y
            return x
        key = jax.random.key(seed)
        ks = jax.random.split(key, 10)
        inp = {'nodes': jax.random.normal(ks[0], (N_NODES, D_NODE), dtype=jnp.float32), 'edges': jax.random.normal(ks[1], (N_EDGES, D_EDGE), dtype=jnp.float32), 'senders': jax.random.randint(ks[2], (N_EDGES,), 0, N_NODES, dtype=jnp.int32), 'receivers': jax.random.randint(ks[3], (N_EDGES,), 0, N_NODES, dtype=jnp.int32), 'W_message': _glorot(ks[4], (D_NODE + D_EDGE, D_NODE)), 'mlp_W0': _glorot(ks[5], (D_NODE, D_NODE)), 'mlp_b0': jnp.zeros((D_NODE,), jnp.float32), 'mlp_W1': _glorot(ks[6], (D_NODE, D_NODE)), 'mlp_b1': jnp.zeros((D_NODE,), jnp.float32), 'mlp_W2': _glorot(ks[7], (D_NODE, D_NODE)), 'mlp_b2': jnp.zeros((D_NODE,), jnp.float32), 'ln_aggr_scale': jnp.ones((D_NODE,), jnp.float32), 'ln_aggr_bias': jnp.zeros((D_NODE,), jnp.float32), 'ln_out_scale': jnp.ones((D_NODE,), jnp.float32), 'ln_out_bias': jnp.zeros((D_NODE,), jnp.float32)}
        return inp
    _L2_gnn_all = _L2_gnn_setup()
    _L2_gnn_in = {k: v for k, v in _L2_gnn_all.items() if k in ('W_message', 'mlp_W0', 'mlp_b0', 'mlp_W1', 'mlp_b1', 'mlp_W2', 'mlp_b2', 'ln_aggr_scale', 'ln_aggr_bias', 'ln_out_scale', 'ln_out_bias')}
    del _L2_gnn_all

    def _L3_gnn_setup():
        import jax, jax.numpy as jnp
        import numpy as np
        N = 3125
        E = 50000
        IN_FEATS = 256
        OUT_FEATS = 256
        MAXK = 32

        def _maxk(x, k):
            _, idx = jax.lax.top_k(x, k)
            rows = jnp.arange(x.shape[0])[:, None]
            mask = jnp.zeros_like(x).at[rows, idx].set(1.0)
            return x * mask
        key = jax.random.key(seed)
        k1, k2, k3, k4, k5 = jax.random.split(key, 5)
        feat = jax.random.normal(k1, (N, IN_FEATS), dtype=jnp.float32)
        W_self = jax.random.normal(k2, (IN_FEATS, OUT_FEATS), dtype=jnp.float32) * (1.0 / np.sqrt(IN_FEATS))
        W_neigh = jax.random.normal(k3, (IN_FEATS, OUT_FEATS), dtype=jnp.float32) * (1.0 / np.sqrt(IN_FEATS))
        src = jax.random.randint(k4, (E,), 0, N, dtype=jnp.int64)
        dst = jax.random.randint(k5, (E,), 0, N, dtype=jnp.int64)
        return {'feat': feat, 'W_self': W_self, 'W_neigh': W_neigh, 'src': src, 'dst': dst}
    _L3_gnn_all = _L3_gnn_setup()
    _L3_gnn_in = {k: v for k, v in _L3_gnn_all.items() if k in ('W_self', 'W_neigh')}
    del _L3_gnn_all
    return {'x': x, 'src': src, 'dst': dst, 'edge_attr_64': edge_attr_64, 'edge_weight': edge_weight, 'L0_gnn_W_l1': _L0_gnn_in['W_l1'], 'L0_gnn_b1': _L0_gnn_in['b1'], 'L0_gnn_W_r1': _L0_gnn_in['W_r1'], 'L0_gnn_W_l2': _L0_gnn_in['W_l2'], 'L0_gnn_b2': _L0_gnn_in['b2'], 'L0_gnn_W_r2': _L0_gnn_in['W_r2'], 'L1_gnn_W': _L1_gnn_in['W'], 'L1_gnn_b': _L1_gnn_in['b'], 'L2_gnn_W_message': _L2_gnn_in['W_message'], 'L2_gnn_mlp_W0': _L2_gnn_in['mlp_W0'], 'L2_gnn_mlp_b0': _L2_gnn_in['mlp_b0'], 'L2_gnn_mlp_W1': _L2_gnn_in['mlp_W1'], 'L2_gnn_mlp_b1': _L2_gnn_in['mlp_b1'], 'L2_gnn_mlp_W2': _L2_gnn_in['mlp_W2'], 'L2_gnn_mlp_b2': _L2_gnn_in['mlp_b2'], 'L2_gnn_ln_aggr_scale': _L2_gnn_in['ln_aggr_scale'], 'L2_gnn_ln_aggr_bias': _L2_gnn_in['ln_aggr_bias'], 'L2_gnn_ln_out_scale': _L2_gnn_in['ln_out_scale'], 'L2_gnn_ln_out_bias': _L2_gnn_in['ln_out_bias'], 'L3_gnn_W_self': _L3_gnn_in['W_self'], 'L3_gnn_W_neigh': _L3_gnn_in['W_neigh']}

def reference(x, src, dst, edge_attr_64, edge_weight, L0_gnn_W_l1, L0_gnn_b1, L0_gnn_W_r1, L0_gnn_W_l2, L0_gnn_b2, L0_gnn_W_r2, L1_gnn_W, L1_gnn_b, L2_gnn_W_message, L2_gnn_mlp_W0, L2_gnn_mlp_b0, L2_gnn_mlp_W1, L2_gnn_mlp_b1, L2_gnn_mlp_W2, L2_gnn_mlp_b2, L2_gnn_ln_aggr_scale, L2_gnn_ln_aggr_bias, L2_gnn_ln_out_scale, L2_gnn_ln_out_bias, L3_gnn_W_self, L3_gnn_W_neigh):
    import jax
    import jax.numpy as jnp

    def _L0_gnn_ref(x, edge_index, W_l1, b1, W_r1, W_l2, b2, W_r2):
        import jax, jax.numpy as jnp
        import numpy as np
        N_NODES = 3125
        N_EDGES = 100000
        D_IN = 256
        D_HID = 256
        D_OUT = 256

        def _sage_conv(x, src, tgt, W_l, b_l, W_r):
            n = x.shape[0]
            msgs = x[src]
            agg = jax.ops.segment_sum(msgs, tgt, num_segments=n)
            deg = jax.ops.segment_sum(jnp.ones((src.shape[0],), x.dtype), tgt, num_segments=n)
            agg = agg / jnp.maximum(deg, 1.0)[:, None]
            return agg @ W_l + b_l + x @ W_r
        src, tgt = (edge_index[0], edge_index[1])
        h = jax.nn.relu(_sage_conv(x, src, tgt, W_l1, b1, W_r1))
        logits = _sage_conv(h, src, tgt, W_l2, b2, W_r2)
        return logits

    def _L1_gnn_ref(x, edge_val, W, b, edge_row, edge_col):
        import jax, jax.numpy as jnp
        import numpy as np
        N_NODES = 3125
        N_EDGES = 100000
        D_IN = 256
        D_OUT = 256
        support = jnp.matmul(x, W)
        gathered = support[edge_col] * edge_val[:, None]
        out = jax.ops.segment_sum(gathered, edge_row, num_segments=x.shape[0])
        return out + b

    def _L2_gnn_ref(nodes, edges, senders, receivers, W_message, mlp_W0, mlp_b0, mlp_W1, mlp_b1, mlp_W2, mlp_b2, ln_aggr_scale, ln_aggr_bias, ln_out_scale, ln_out_bias):
        import jax, jax.numpy as jnp
        import numpy as np
        N_NODES = 50000
        N_EDGES = 12500
        D_NODE = 256
        D_EDGE = 64
        LN_EPS = 1e-06

        def _layer_norm(x, scale, bias):
            mu = jnp.mean(x, axis=-1, keepdims=True)
            var = jnp.mean(jnp.square(x - mu), axis=-1, keepdims=True)
            return (x - mu) * jax.lax.rsqrt(var + LN_EPS) * scale + bias

        def _glorot(key, shape):
            fan_in, fan_out = shape
            std = jnp.sqrt(2.0 / (fan_in + fan_out))
            return std * jax.random.normal(key, shape, dtype=jnp.float32)

        def _relu_mlp_skip(x, Ws, bs):
            n = len(Ws)
            for i, (W, b) in enumerate(zip(Ws, bs)):
                y = x @ W + b
                if i < n - 1:
                    y = jax.nn.relu(y)
                x = x + y if y.shape[-1] == x.shape[-1] else y
            return x
        total_nodes = nodes.shape[0]
        sender_features = nodes[senders]
        msg_in = jnp.concatenate([sender_features, edges], axis=-1)
        messages = msg_in @ W_message
        agg = jax.ops.segment_sum(messages, receivers, num_segments=total_nodes)
        h = _layer_norm(jax.nn.relu(agg) + nodes, ln_aggr_scale, ln_aggr_bias)
        nodes_out = _relu_mlp_skip(h, [mlp_W0, mlp_W1, mlp_W2], [mlp_b0, mlp_b1, mlp_b2])
        nodes_new = _layer_norm(nodes + nodes_out, ln_out_scale, ln_out_bias)
        return nodes_new

    def _L3_gnn_ref(feat, W_self, W_neigh, src, dst):
        import jax, jax.numpy as jnp
        import numpy as np
        N = 3125
        E = 50000
        IN_FEATS = 256
        OUT_FEATS = 256
        MAXK = 32

        def _maxk(x, k):
            _, idx = jax.lax.top_k(x, k)
            rows = jnp.arange(x.shape[0])[:, None]
            mask = jnp.zeros_like(x).at[rows, idx].set(1.0)
            return x * mask
        n = feat.shape[0]
        h_self = feat @ W_self
        h_neigh = feat @ W_neigh
        h_sparse = _maxk(h_neigh, MAXK)
        msg = h_sparse[src]
        summed = jax.ops.segment_sum(msg, dst, num_segments=n)
        deg = jax.ops.segment_sum(jnp.ones((src.shape[0],), dtype=feat.dtype), dst, num_segments=n)
        neigh = summed / jnp.maximum(deg, 1.0)[:, None]
        return h_self + neigh
    edge_index = jnp.stack([src, dst])
    h = jnp.maximum(_layernorm(x, axis=-1), 0.0)
    x = x + _L0_gnn_ref(h, edge_index, L0_gnn_W_l1, L0_gnn_b1, L0_gnn_W_r1, L0_gnn_W_l2, L0_gnn_b2, L0_gnn_W_r2)
    h = jnp.maximum(_layernorm(x, axis=-1), 0.0)
    x = x + _L1_gnn_ref(h, edge_weight, L1_gnn_W, L1_gnn_b, src, dst)
    h = jnp.maximum(_layernorm(x, axis=-1), 0.0)
    x = x + _L2_gnn_ref(h, edge_attr_64, src, dst, L2_gnn_W_message, L2_gnn_mlp_W0, L2_gnn_mlp_b0, L2_gnn_mlp_W1, L2_gnn_mlp_b1, L2_gnn_mlp_W2, L2_gnn_mlp_b2, L2_gnn_ln_aggr_scale, L2_gnn_ln_aggr_bias, L2_gnn_ln_out_scale, L2_gnn_ln_out_bias)
    h = jnp.maximum(_layernorm(x, axis=-1), 0.0)
    x = x + _L3_gnn_ref(h, L3_gnn_W_self, L3_gnn_W_neigh, src, dst)
    return x

_drawn_inputs = setup_inputs


def setup_inputs(seed=0):
    import zlib

    import numpy as np

    out = dict(_drawn_inputs(seed))
    spreads = {'L0_gnn_b1': (0.0, 0.1),
     'L0_gnn_b2': (0.0, 0.1),
     'L2_gnn_mlp_b0': (0.0, 0.41),
     'L2_gnn_mlp_b1': (0.0, 0.571),
     'L2_gnn_mlp_b2': (0.0, 0.542),
     'L2_gnn_ln_aggr_scale': (1.0, 0.2),
     'L2_gnn_ln_aggr_bias': (0.0, 0.1),
     'L2_gnn_ln_out_scale': (1.0, 0.2),
     'L2_gnn_ln_out_bias': (0.0, 0.1)}
    factors = {'L1_gnn_b': 3.655}
    for name, (base, spread) in spreads.items():
        noise = np.random.default_rng([zlib.crc32(name.encode()), seed]).standard_normal(out[name].shape)
        drawn = base * np.exp(spread * noise) if base else spread * noise
        out[name] = jnp.asarray(drawn.astype(out[name].dtype))
    for name, factor in factors.items():
        out[name] = (out[name] * factor).astype(out[name].dtype)
    return out
```

```python
from contextlib import ExitStack

import numpy as np
import concourse.bass as bass
from concourse import mybir
from concourse.alu_op_type import AluOpType as ALU

F32, F16, BF16, I32 = mybir.dt.float32, mybir.dt.float16, mybir.dt.bfloat16, mybir.dt.int32
ACT = mybir.ActivationFunctionType
AX = mybir.AxisListType

P = 128
N, D, E, DE = 3125, 256, 50000, 64
NT = -(-N // P)
NR = N - (NT - 1) * P
ET = -(-E // P)
ER = E - (ET - 1) * P
EB = -(-ET // P)
G = 16
PER = P // G
NG = NT * PER
GW = NT * G
SG = P // G
TOPK = 32
PAD_DST = 4095
ZW = 3 * D + 2
RING = 4
SETW = 2 * GW + 4 * P
EPW = 3 * DE
EBLK = 8
NPAIR = NT // 2
CR = 2
PH_PRE, PH_SAGE1, PH_SAGE2, PH_GCN, PH_INTER, PH_MAXK = range(6)
LN_EPS, LN_EPS_INTER = 1e-5, 1e-6
LOWEST = -3.4e38
PREP_ROWS = 17 + 7 + 4
PREP_SCAN = PREP_ROWS + 6 + 8 + 4
PREP_STEPS = PREP_SCAN + 14 + 4 + 7 + 1


def build(nc, x, src, dst, edge_attr, edge_weight, w, out):
    ctx = ExitStack()
    with ctx:
        def sb(name, shape, dt):
            return ctx.enter_context(nc.sbuf_tensor(name, shape, dt))

        def sem(name):
            return ctx.enter_context(nc.semaphore(name))

        cnt_dram = nc.dram_tensor("cnt_blocks", (NT, P, NT * P), F16, kind="Internal").ap()
        wgt_dram = nc.dram_tensor("wgt_blocks", (NT * P, NT * P), F32, kind="Internal").ap()
        ea_dram = nc.dram_tensor("edge_sums", (NT, P, DE), F32, kind="Internal").ap()

        XW, ZF = NT * D, NT * ZW // 2
        BLKF = NT * P
        arena = sb("arena", [P, 2 * XW + 2 * ZF + 2 * BLKF], F32)

        def region(at, words):
            return arena[:, at:at + words]

        o_r, o_z0, o_z1, o_blk = XW, 2 * XW, 2 * XW + ZF, 2 * XW + 2 * ZF
        X = region(0, XW).rearrange("p (n d) -> p n d", d=D)
        R_ = region(o_r, XW).rearrange("p (n d) -> p n d", d=D)
        Z = [region(o, ZF).bitcast(BF16) for o in (o_z0, o_z1)]
        ZFULL = [region(o, XW) for o in (o_z0, o_z1)]
        BLK32 = [region(o_blk + b * BLKF, BLKF) for b in range(2)]
        BLK16 = [region(o_blk + b * BLKF, BLKF // 2).bitcast(F16) for b in range(2)]
        EP = region(0, ET * EPW // 2).bitcast(BF16)
        rows = region(0, 3 * EB * P).rearrange("p (a c e) -> p a c e", a=3, c=EB)
        rows_i = rows.bitcast(I32)
        ROW0 = 3 * EB * P
        part_i = region(ROW0, 3 * EB * P).bitcast(I32).rearrange("p (a c e) -> p a c e", a=3, c=EB)
        part_f = region(2 * ROW0, 9 * EB * P).rearrange("p (a c e) -> p a c e", a=9, c=EB)
        stage_c = [region(o_z1 + b * BLKF // 2, BLKF // 2).bitcast(F16).rearrange("p (b d) -> p b d", d=P)
                   for b in range(2)]
        stage_w = [region(o_z1 + BLKF + b * BLKF, BLKF).rearrange("p (t s) -> p t s", s=GW) for b in range(2)]

        NCOL = EB * P
        front = sb("front", [P, 8 * NCOL + RING * SETW // 2], F32)
        col = front[:, 0:8 * NCOL].rearrange("p (a t) -> p a t", a=8)
        C_KEY, C_DST, C_SRC, C_W0, C_KEYW, C_REM, C_W1, C_W2 = range(8)
        ring = front[:, 8 * NCOL:].bitcast(BF16)
        late = {}
        at = 0
        for name, width in (("W_gcn", 2 * D), ("W_msg", 2 * D), ("W_maxk", 4 * D), ("mlp0", 2 * D), ("mlp1", 2 * D),
                            ("mlp2", 2 * D), ("W_edge", D), ("b_gcn", D), ("s_out", D), ("b_out", D)):
            late[name] = front[:, at:at + width]
            at += width

        def wk(ap, n):
            return ap.rearrange("p (k n) -> p k n", n=n)

        W_early = sb("W_early", [P, 2, 2, 2 * D], F32)
        b_early = sb("b_early", [P, 2, D], F32)
        mlp_col = sb("mlp_col", [P, 5, 2], F32)
        ident = sb("ident", [P, P], F32)
        iota1 = sb("iota1", [P, GW], F16)
        off_g = sb("off_g", [P, NG], F32)
        off_c = sb("off_c", [P, NG], F32)
        nidx = sb("nidx", [P, 2], F32)
        zeros = sb("zeros", [P, P], BF16)
        ones_row = sb("ones_row", [1, P], F32)
        work = sb("work", [P, 12, D], F32)
        hrow = [work[:, b, :] for b in range(2)]
        hT = [work[:, 2 + b, :] for b in range(2)]
        resid = [work[:, 4 + b, :] for b in range(2)]
        GT = work[:, 6:8, :]
        YT = work[:, 8, :]
        urow = work[:, 9, :]
        inner_row, keep = work[:, 10, :], work[:, 11, :]
        count_scratch = work[:, 8:10, :].rearrange("p a d -> p (a d)")[:, 0:ET]
        raw = [work[:, 2 * b:2 * b + 2, :].rearrange("p a (t f) -> p (a t) f", f=DE) for b in range(2)]
        raw_rest = work[:, 4:6, :].rearrange("p a (t f) -> p (a t) f", f=DE)
        ea3 = work[:, 6:8, :].rearrange("p a d -> p (a d)")[:, 0:2 * EPW]
        ea_sum = [work[:, 11, b * DE:(b + 1) * DE] for b in range(2)]
        small = sb("small", [P, 32], F32)
        keyrel = small[:, 24:24 + RING]
        bn, mv, ve, sd, rs, mx8 = (small[:, 0:6], small[:, 6:8], small[:, 8:9], small[:, 9:10], small[:, 10:11],
                                   small[:, 16:24])
        rdeg = sb("rdeg", [P, NT], F32)
        stat = sb("stat", [P, 4, EB], F32)
        scan = work[0:1, 4:8, :].rearrange("o (a b) d -> o a (b d)", a=2)
        tab_f = sb("tab_f", [P, 16], F32)
        tab = sb("tab", [1, 3 * P], I32)
        ea_now = sb("ea_now", [P, P], F32)
        eaT = sb("eaT", [DE, P], F32)

        ps = ctx.enter_context(nc.psum_tensor("ps", [P, 8, 512], F32))
        agg = [ps[:, b, :] for b in range(2)]
        tp = [ps[:, 2 + b, 0:D] for b in range(2)]
        mmo = [ps[:, 4 + b, :] for b in range(2)]
        mlp_ps = ps[:, 6, 0:D]
        tv, tb = ps[:, 7, 0:D], ps[:, 7, D:2 * D]
        cnt_ps = [ps[:, b, :] for b in range(2)]
        wgt_ps = [ps[:, 2 + b, :] for b in range(2)]

        s_const = sem("constants_ready")
        s_rows = sem("edge_rows_loaded")
        s_pad = sem("padding_set")
        s_prep = sem("dve_prep_step")
        s_prep_pe = sem("pe_prep_step")
        s_raw = [sem(f"edge_features_loaded{b}") for b in range(2)]
        s_e0 = sem("edge_first_part")
        s_erest = sem("edge_rest")
        s_e12 = sem("edge_other_parts")
        s_onehot = sem("onehots_ready")
        s_used = sem("onehots_used")
        s_built = sem("tile_built")
        s_taken = sem("built_tile_taken")
        s_ea = sem("edge_sums_copied")
        s_ea2 = sem("edge_sums_added")
        s_eastore = [sem(f"edge_sums_stored{b}") for b in range(2)]
        s_store_c = [sem(f"count_block_stored{b}") for b in range(2)]
        s_store_w = [sem(f"weight_block_stored{b}") for b in range(2)]
        s_w = sem("early_weights_loaded")
        s_wlate = sem("late_weights_loaded")
        s_x = sem("x_loaded")
        s_xpad = sem("x_padding_set")
        s_blk = [sem(f"block_loaded{b}") for b in range(2)]
        s_agg = sem("aggregated")
        s_aggfree = sem("aggregate_read")
        s_var = sem("variance_ready")
        s_std = sem("deviation_ready")
        s_row = sem("rows_normalised")
        s_tp = sem("rows_transposed")
        s_hT = sem("transpose_copied")
        s_mm = sem("rows_multiplied")
        s_z0 = sem("first_part_ready")
        s_zD = sem("rest_ready")
        s_z2 = sem("parts_ready")
        s_inner = sem("inner_norm_ready")
        s_tv = sem("inner_rows_transposed")
        s_g0 = sem("inner_rows_copied")
        s_q = sem("mlp_layer_multiplied")
        s_y = sem("mlp_layer_activated")
        s_g = sem("mlp_layer_added")
        s_tb = sem("mlp_rows_back")
        s_ean = sem("edge_sums_at_hand")
        s_eat = sem("edge_sums_transposed")
        s_eac = sem("edge_transpose_copied")
        s_done = sem("rows_final")
        s_out = sem("output_stored")

        block = ctx.enter_context(nc.Block())

        def wait(e, s, v):
            e.wait_ge(s, v if isinstance(v, int) else e.snap(v))

        class Chain:

            def __init__(self, e, s):
                self.e, self.s, self.v = e, s, 0

            def __call__(self, ins):
                ins.then_inc(self.s, 1)
                self.v += 1
                self.e.wait_ge(self.s, self.v)

        def drained(e):
            def step(ins):
                e.drain()
            return step

        def tiles(e, phase, body, first=0):
            k0 = NT * phase + first
            with e.Fori(0, (NT - first) // 2) as j:
                for c in range(2):
                    body(j * 2 + (first + c), j * 2 + (k0 + c), j + (k0 + c) // 2, (k0 + c) % 2)
            if (NT - first) % 2:
                g = NT * phase + NT - 1
                body(NT - 1, g, g // 2, g % 2)

        def one(ap, n):
            return ap[:, n:n + 1] if isinstance(n, int) else ap[:, bass.ds(n, 1)]

        def span(ap, start, width):
            return ap[:, start:start + width] if isinstance(start, int) else ap[:, bass.ds(start, width)]

        def node(ap, n):
            return ap[:, n, :] if isinstance(n, int) else ap[:, bass.ds(n, 1), :].rearrange("p a d -> p (a d)")

        def bounded(v, low, high):
            return nc.s_assert_within(v, low, high, skip_runtime_bounds_check_because="the table is clamped to it")

        def edge_range(e, i):
            v = e.value_load(tab[0:1, i:i + 1] if isinstance(i, int) else tab[0:1, bass.ds(i, 1)],
                             min_val=1, max_val=(ET - 1) * 512 + ET)
            return (bounded(e.snap(v >> 9), 0, ET - 1), bounded(e.snap(v & 511), 1, ET))

        T_CHUNK = 2 * P

        def zin(i):
            return i % 2

        @block.sync
        def _(sp):
            sp.wait_ge(s_pad, 3)
            full = (E // P) // P * P
            for a, t in enumerate((src, dst, edge_weight)):
                into = rows_i if a < 2 else rows
                for c in range(EB - 1):
                    sp.dma_start(into[:, a, c, :], t[c * P * P:(c + 1) * P * P].rearrange("(p e) -> p e", e=P)
                                 ).then_inc(s_rows, 16)
                sp.dma_start(into[0:ET - 1 - full, a, EB - 1, :],
                             t[full * P:(ET - 1) * P].rearrange("(p e) -> p e", e=P)).then_inc(s_rows, 16)
                sp.dma_start(into[ET - 1 - full:ET - full, a, EB - 1, 0:ER],
                             t[(ET - 1) * P:E].rearrange("(p e) -> p e", p=1)).then_inc(s_rows, 16)
            for i, (l, r, b) in enumerate((("W_l1", "W_r1", "b1"), ("W_l2", "W_r2", "b2"))):
                for h, name in enumerate((l, r)):
                    sp.dma_start(W_early[:, i, :, h * D:(h + 1) * D],
                                 w["L0_gnn_" + name].rearrange("(k p) n -> p k n", p=P)).then_inc(s_w, 16)
                sp.dma_start(b_early[:, i, :], w["L0_gnn_" + b].rearrange("(o n) -> o n", o=1).broadcast_to([P, D])
                             ).then_inc(s_w, 16)
            for i, name in enumerate(("mlp_b0", "mlp_b1", "mlp_b2", "ln_aggr_scale", "ln_aggr_bias")):
                for k in range(2):
                    sp.dma_start(mlp_col[:, i, k:k + 1],
                                 w["L2_gnn_" + name][k * P:(k + 1) * P].rearrange("(p o) -> p o", o=1)
                                 ).then_inc(s_w, 16)

            def features(t0, par, use):
                wait(sp, s_e12, use)
                sp.dma_start(raw[par], edge_attr[bass.ds(t0 * P, EBLK * P), :].rearrange("(t p) f -> p t f", p=P)
                             ).then_inc(s_raw[par], 16)

            sp.wait_ge(s_prep_pe, 28)
            with sp.Fori(0, ET // EBLK // 2) as j:
                for c in range(2):
                    features((j * 2 + c) * EBLK, c, j * 2 + c + 1)
            t0 = ET // EBLK * EBLK
            sp.wait_ge(s_e12, ET // EBLK + 1)
            sp.wait_ge(s_pad, 4)
            sp.dma_start(raw[0][:, 0:ET - 1 - t0, :],
                         edge_attr[t0 * P:(ET - 1) * P, :].rearrange("(t p) f -> p t f", p=P)).then_inc(s_raw[0], 16)
            sp.dma_start(raw[0][0:ER, ET - 1 - t0, :], edge_attr[(ET - 1) * P:E, :]).then_inc(s_raw[0], 16)

            def store_sums(c, g, h, par):
                wait(sp, s_ea2, c + 1 + CR)
                sp.dma_start(ea_dram[c] if isinstance(c, int) else
                             ea_dram[bass.ds(c, 1)].rearrange("o p f -> (o p) f"), ea_sum[par]
                             ).then_inc(s_eastore[par], 16)
            tiles(sp, 0, store_sums)

            sp.wait_ge(s_xpad, 2)
            sp.dma_start(X[:, 0:NT - 1, :], x[0:(NT - 1) * P, :].rearrange("(n p) d -> p n d", p=P)).then_inc(s_x, 16)
            sp.dma_start(X[0:NR, NT - 1, :], x[(NT - 1) * P:N, :]).then_inc(s_x, 16)

            def store(c, half, par):
                wait(sp, s_taken, c * PER + (PER + CR))
                dc = cnt_dram[c] if isinstance(c, int) else cnt_dram[bass.ds(c, 1)].rearrange("o p f -> (o p) f")
                rows_of = wgt_dram[bass.ds(c * P, P), :]
                sp.dma_start(dc, stage_c[par].rearrange("p b d -> p (b d)")).then_inc(s_store_c[par], 16)
                sp.dma_start(rows_of.rearrange("(t d) (g s) -> (d g) t s", d=G, g=SG), stage_w[par]
                             ).then_inc(s_store_w[par], 16)

            with sp.Fori(0, NPAIR) as j:
                for c in range(2):
                    store(j * 2 + c, j, c)
            store(NT - 1, NPAIR, 0)

            sp.wait_ge(s_built, NT + NG)
            for name, of in (("W_gcn", "L1_gnn_W"), ("mlp0", "L2_gnn_mlp_W0"), ("mlp1", "L2_gnn_mlp_W1"),
                             ("mlp2", "L2_gnn_mlp_W2")):
                sp.dma_start(wk(late[name], D), w[of].rearrange("(k p) n -> p k n", p=P)).then_inc(s_wlate, 16)
            sp.dma_start(wk(late["W_msg"], D), w["L2_gnn_W_message"][0:D, :].rearrange("(k p) n -> p k n", p=P)
                         ).then_inc(s_wlate, 16)
            sp.dma_start(late["W_edge"][0:DE, :], w["L2_gnn_W_message"][D:D + DE, :]).then_inc(s_wlate, 16)
            for h, of in enumerate(("L3_gnn_W_neigh", "L3_gnn_W_self")):
                sp.dma_start(wk(late["W_maxk"], 2 * D)[:, :, h * D:(h + 1) * D],
                             w[of].rearrange("(k p) n -> p k n", p=P)).then_inc(s_wlate, 16)
            for name, of in (("b_gcn", "L1_gnn_b"), ("s_out", "L2_gnn_ln_out_scale"), ("b_out", "L2_gnn_ln_out_bias")):
                sp.dma_start(late[name], w[of].rearrange("(o n) -> o n", o=1).broadcast_to([P, D])
                             ).then_inc(s_wlate, 16)

            for par in range(2):
                uses = (NT + 1 - par) // 2
                sp.wait_ge(s_store_c[par], 16 * uses)
                sp.wait_ge(s_store_w[par], 16 * uses)
            for i in range(5):
                def load(n, q, h, par, i=i):
                    wait(sp, s_agg, q + 1)
                    if i == 2:
                        cols = wgt_dram[:, bass.ds(n * P, P)].rearrange("(b p) s -> p b s", p=P)
                        sp.dma_start(BLK32[par].rearrange("p (b s) -> p b s", s=P), cols).then_inc(s_blk[par], 16)
                    else:
                        f = cnt_dram[n] if isinstance(n, int) else \
                            cnt_dram[bass.ds(n, 1)].rearrange("o p f -> (o p) f")
                        sp.dma_start(BLK16[par], f).then_inc(s_blk[par], 16)
                    if i == 3:
                        wait(sp, s_eat, n)
                        f = ea_dram[n] if isinstance(n, int) else \
                            ea_dram[bass.ds(n, 1)].rearrange("o p f -> (o p) f")
                        sp.dma_start(ea_now[:, 0:DE], f).then_inc(s_ean, 16)
                tiles(sp, i, load)

            def store_out(n, g, h, par):
                wait(sp, s_done, n + 1)
                sp.dma_start(out[bass.ds(n * P, P), :], node(X, n)).then_inc(s_out, 16)

            with sp.Fori(0, NT - 1) as n:
                store_out(n, 0, 0, 0)
            sp.wait_ge(s_done, NT)
            sp.dma_start(out[(NT - 1) * P:N, :], X[0:NR, NT - 1, :]).then_inc(s_out, 16)
            sp.wait_ge(s_out, 16 * NT)

        @block.gpsimd
        def _(pool):
            chain = drained(pool)
            pool.memset(rows_i[:, 0, EB - 1, :], 0).then_inc(s_pad, 1)
            pool.memset(rows_i[:, 1, EB - 1, :], PAD_DST).then_inc(s_pad, 1)
            pool.memset(rows[:, 2, EB - 1, :], 0.0).then_inc(s_pad, 1)
            chain(pool.memset(ident[:, :], 0.0))
            pool.affine_select(out=ident[:, :], in_=ident[:, :], compare_op=ALU.not_equal, fill=1.0, base=0,
                               pattern=[[-1, P]], channel_multiplier=1).then_inc(s_const, 1)
            pool.iota(iota1[:, :], pattern=[[1, GW]], base=1, channel_multiplier=0,
                      allow_small_or_imprecise_dtypes=True).then_inc(s_const, 1)
            pool.iota(off_g[:, :], pattern=[[GW, NG]], base=0, channel_multiplier=0,
                      allow_small_or_imprecise_dtypes=True).then_inc(s_const, 1)
            pool.iota(off_c[:, :], pattern=[[P, NG]], base=0, channel_multiplier=0,
                      allow_small_or_imprecise_dtypes=True).then_inc(s_const, 1)
            pool.iota(nidx[:, :], pattern=[[P, 2]], base=0, channel_multiplier=1,
                      allow_small_or_imprecise_dtypes=True).then_inc(s_const, 1)
            pool.memset(zeros[:, :], 0.0).then_inc(s_const, 1)
            pool.memset(ea_now[:, :], 0.0)
            pool.memset(ones_row[:, :], 1.0).then_inc(s_const, 1)
            pool.sem_inc(s_e12, CR)
            pool.sem_inc(s_z2, CR)

            def parts(t0, tiles_, use, v):
                wait(pool, s_erest, use)
                rest = raw_rest[:, 0:tiles_, :]
                ep = span(EP, t0 * EPW, tiles_ * EPW).rearrange("p (t k f) -> p t k f", k=3, f=DE)
                chain(pool.tensor_copy(ep[:, :, 1, :], rest))
                pool.tensor_tensor(ep[:, :, 2, :], rest, ep[:, :, 1, :], ALU.subtract).then_inc(s_e12, 1)

            with pool.Fori(0, ET // EBLK // 2) as j:
                for c in range(2):
                    parts((j * 2 + c) * EBLK, EBLK, j * 2 + c + 1, None)
            pool.wait_ge(s_e12, ET // EBLK + CR)
            pool.memset(raw[0][:, ET % EBLK - 1, :], 0.0).then_inc(s_pad, 1)
            parts(ET // EBLK * EBLK, ET % EBLK, ET // EBLK + 1, None)

            def add_parts(c, g, h, par):
                wait(pool, s_ea, c + 1 + CR)
                three = ea3[:, par * EPW:(par + 1) * EPW].rearrange("p (k f) -> p k f", k=3)
                wait(pool, s_eastore[par], h * 16)
                chain(pool.tensor_tensor(ea_sum[par], three[:, 1, :], three[:, 2, :], ALU.add))
                pool.tensor_tensor(ea_sum[par], ea_sum[par], three[:, 0, :], ALU.add).then_inc(s_ea2, 1)
            tiles(pool, 0, add_parts)

            pool.wait_ge(s_built, NT)
            pool.memset(X[:, NT - 1, :], 0.0).then_inc(s_xpad, 1)
            pool.memset(Z[0].rearrange("p (n k) -> p n k", k=ZW)[:, :, 3 * D:ZW], 1.0).then_inc(s_xpad, 1)

            def split(n, g, h, par, zo):
                wait(pool, s_zD, g + 1 + CR)
                z1, z2 = (span(Z[zo], n * ZW + k * D, D) for k in (1, 2))
                chain(pool.tensor_copy(z1, resid[par]))
                pool.tensor_tensor(z2, resid[par], z1, ALU.subtract).then_inc(s_z2, 1)

            tiles(pool, PH_PRE, lambda n, g, h, par: split(n, g, h, par, 0))
            tiles(pool, PH_SAGE1, lambda n, g, h, par: split(n, g, h, par, 1))

            def none(n, g, h, par):
                wait(pool, s_zD, g + 1 + CR)
                pool.sem_inc(s_z2, 1)
            tiles(pool, PH_SAGE2, none)
            tiles(pool, PH_GCN, lambda n, g, h, par: split(n, g, h, par, 1))

            def mlp_sums(n):
                for l in range(3):
                    wait(pool, s_y, n * 3 + (l + 1))
                    pool.tensor_tensor(GT[:, (l + 1) % 2, :], GT[:, l % 2, :], YT, ALU.add).then_inc(s_g, 1)

            mlp_sums(0)
            mlp_sums(1)
            g0 = NT * PH_INTER

            with pool.Fori(0, NPAIR - 1) as j:
                for c in range(2):
                    split(j * 2 + c, j * 2 + (g0 + c), None, (g0 + c) % 2, 0)
                    mlp_sums(j * 2 + (c + 2))
            for n in range(2 * (NPAIR - 1), NT):
                split(n, g0 + n, None, (g0 + n) % 2, 0)
                if n + 2 < NT:
                    mlp_sums(n + 2)

        @block.scalar
        def _(act):
            act.sem_inc(s_hT, CR)
            act.sem_inc(s_z0, CR)
            act.sem_inc(s_taken, CR)

            def first_part(t0, n, par, uses, use):
                wait(act, s_raw[par], uses * 16)
                ep = span(EP, t0 * EPW, n * EPW).rearrange("p (t k f) -> p t k f", k=3, f=DE)
                act.activation(ep[:, :, 0, :], raw[par][:, 0:n, :], ACT.Copy).then_inc(s_e0, 1)
            with act.Fori(0, ET // EBLK // 2) as j:
                for c in range(2):
                    first_part((j * 2 + c) * EBLK, EBLK, c, j + 1, None)
            first_part(ET // EBLK * EBLK, ET % EBLK, 0, ET // EBLK // 2 + 2, None)

            def take_edges(c, g, h, par):
                wait(act, s_built, c + 1)
                wait(act, s_ea2, c - 1 + CR)
                act.activation(ea3[:, par * EPW:(par + 1) * EPW], cnt_ps[par][:, 0:EPW], ACT.Copy
                               ).then_inc(s_ea, 1)
            act.sem_inc(s_ea2, CR)
            act.sem_inc(s_ea, CR)
            tiles(act, 0, take_edges)

            def deviation(k):
                wait(act, s_var, k + 1)
                act.activation(sd, ve, ACT.Sqrt).then_inc(s_std, 1)

            def copy_transpose(g, par):
                wait(act, s_tp, g + 1 + CR)
                wait(act, s_mm, g - 1 + CR)
                act.activation(hT[par], tp[par], ACT.Relu).then_inc(s_hT, 1)

            def first_z(n, g, par, zo):
                wait(act, s_mm, g + 1 + CR)
                act.activation(span(Z[zo], n * ZW, D), mmo[par][:, 0:D], ACT.Copy).then_inc(s_z0, 1)

            def row_phase(phase, z, ln):
                g0 = NT * phase
                if ln is not None:
                    deviation(ln)
                copy_transpose(g0, g0 % 2)

                def body(n, g, h, par):
                    if ln is not None:
                        deviation(n + ln)
                    z(n - 1, g - 1, 1 - par)
                    copy_transpose(g, par)
                tiles(act, phase, body, first=1)
                z(NT - 1, g0 + NT - 1, (g0 + NT - 1) % 2)

            row_phase(PH_PRE, lambda n, g, par: first_z(n, g, par, 0), 0)

            def take(c, half, par):
                if par is not None:
                    wait(act, s_store_c[par], half * 16)
                    wait(act, s_store_w[par], half * 16)
                for t in range(PER):
                    wait(act, s_built, c * PER + (NT + t + 1))
                    act.activation(stage_c[par][:, :, t * G:(t + 1) * G],
                                   cnt_ps[t % 2][:, 0:GW].rearrange("p (b d) -> p b d", d=G), ACT.Copy)
                    a = act.activation(stage_w[par][:, t, :], wgt_ps[t % 2][:, 0:GW], ACT.Copy)
                    a.then_inc(s_taken, 1)
            with act.Fori(0, NPAIR) as j:
                for c in range(2):
                    take(j * 2 + c, j, c)
            take(NT - 1, NPAIR, 0)

            row_phase(PH_SAGE1, lambda n, g, par: first_z(n, g, par, 1), None)

            def whole_z(n, g, par):
                wait(act, s_mm, g + 1 + CR)
                act.activation(span(ZFULL[0], n * D, D), mmo[par][:, 0:D], ACT.Copy).then_inc(s_z0, 1)
            row_phase(PH_SAGE2, whole_z, NT)
            row_phase(PH_GCN, lambda n, g, par: first_z(n, g, par, 1), 2 * NT)

            g0, ln0 = NT * PH_INTER, 3 * NT

            def mlp(n):
                wait(act, s_tv, n + 1)
                for k in range(2):
                    a = act.activation(GT[:, 0, k * P:(k + 1) * P], tv[:, k * P:(k + 1) * P], ACT.Identity,
                                       bias=mlp_col[:, 4, k:k + 1], scale=mlp_col[:, 3, k:k + 1])
                a.then_inc(s_g0, 1)
                for l in range(3):
                    wait(act, s_q, n * 3 + (l + 1))
                    for k in range(2):
                        a = act.activation(YT[:, k * P:(k + 1) * P], mlp_ps[:, k * P:(k + 1) * P],
                                           ACT.Relu if l < 2 else ACT.Identity, bias=mlp_col[:, l, k:k + 1])
                    a.then_inc(s_y, 1)

            def edge_copy(n):
                wait(act, s_eat, n + 1)
                act.activation(eaT[:, :], mlp_ps[0:DE, 0:P], ACT.Copy).then_inc(s_eac, 1)

            def inter(n, g, par, back2=True, back1=True, here=True):
                if here:
                    edge_copy(n)
                if back2:
                    copy_transpose(g - 2, par)
                if back1:
                    mlp(n - 1)
                if here:
                    deviation(n * 3 + (ln0 - (0 if isinstance(n, int) and n == 0 else 2)))
                if back1:
                    last = isinstance(n, int) and n == NT
                    deviation(n * 3 + (ln0 - (2 if last else 1)) if not last else ln0 + 3 * NT - 2)
                    deviation(n * 3 + ln0 if not last else ln0 + 3 * NT - 1)
                if back2:
                    wait(act, s_mm, g - 1 + CR)
                    act.sem_inc(s_z0, 1)
            inter(0, g0, g0 % 2, False, False)
            inter(1, g0 + 1, (g0 + 1) % 2, False)
            with act.Fori(0, (NT - 3) // 2) as j:
                for c in range(2):
                    inter(j * 2 + (2 + c), j * 2 + (g0 + 2 + c), (g0 + c) % 2)
            inter(NT - 1, g0 + NT - 1, (g0 + NT - 1) % 2)
            inter(NT, g0 + NT, (g0 + NT) % 2, here=False)
            inter(NT + 1, g0 + NT + 1, (g0 + NT + 1) % 2, back1=False, here=False)

        @block.vector
        def _(dve):
            chain = Chain(dve, s_prep)
            dve.wait_ge(s_rows, 16 * 3 * (EB + 1))
            dve.wait_ge(s_pad, 3)
            dve.wait_ge(s_const, 7)
            whole = "p c e -> p (c e)"
            S, Dd, Wt = (rows_i[:, 0].rearrange(whole), rows_i[:, 1].rearrange(whole), rows[:, 2].rearrange(whole))
            pi = [part_i[:, a].rearrange(whole) for a in range(3)]
            pf = [part_f[:, a].rearrange(whole) for a in range(9)]
            dve.tensor_scalar(pi[0], S, 7, 4, ALU.arith_shift_right, ALU.logical_shift_left).then_inc(s_prep, 1)
            dve.tensor_scalar(pi[1], S, 127, None, ALU.bitwise_and).then_inc(s_prep, 1)
            dve.tensor_scalar(pi[2], Dd, 4, None, ALU.arith_shift_right).then_inc(s_prep, 1)
            dve.wait_ge(s_prep, 3)
            chain.v = 3
            dve.tensor_copy(pf[3], pi[0]).then_inc(s_prep, 1)
            dve.tensor_scalar(pf[2], pi[1], 1.0, None, ALU.add).then_inc(s_prep, 1)
            dve.tensor_copy(pf[4], pi[2]).then_inc(s_prep, 1)
            dve.tensor_scalar(pf[1], Dd, 1.0, None, ALU.add).then_inc(s_prep, 1)
            dve.wait_ge(s_prep, 7)
            dve.tensor_scalar(pi[0], Dd, 7, None, ALU.arith_shift_right).then_inc(s_prep, 1)
            dve.tensor_scalar(pi[1], Dd, G - 1, None, ALU.bitwise_and).then_inc(s_prep, 1)
            dve.scalar_tensor_tensor(out=pf[0], in0=pf[4], scalar=float(GW), in1=pf[3], op0=ALU.mult, op1=ALU.add
                                     ).then_inc(s_prep, 1)
            dve.wait_ge(s_prep, 10)
            dve.tensor_copy(pf[5], pi[0]).then_inc(s_prep, 1)
            dve.tensor_copy(pf[3], pi[1]).then_inc(s_prep, 1)
            dve.wait_ge(s_prep, 12)
            dve.scalar_tensor_tensor(out=pf[0], in0=pf[3], scalar=1.0, in1=pf[0], op0=ALU.add, op1=ALU.add
                                     ).then_inc(s_prep, 1)
            chain.v = 13
            chain(dve.tensor_scalar(pf[6], S, float(GW), None, ALU.is_ge))
            for g in range(2, SG):
                chain(dve.scalar_tensor_tensor(out=pf[6], in0=S, scalar=float(GW * g), in1=pf[6], op0=ALU.is_ge,
                                               op1=ALU.add))
            chain(dve.tensor_scalar(pf[7], S, 1.0, None, ALU.add))
            chain(dve.scalar_tensor_tensor(out=pf[7], in0=pf[6], scalar=-float(GW), in1=pf[7], op0=ALU.mult,
                                           op1=ALU.add))
            chain(dve.tensor_scalar(pf[8], Dd, float(SG), 1.0, ALU.mult, ALU.add))
            chain(dve.tensor_tensor(pf[8], pf[8], pf[6], ALU.add))
            for a, (f, op) in enumerate(((4, ALU.max), (4, ALU.min), (5, ALU.max), (5, ALU.min))):
                dve.tensor_reduce(stat[:, a, :], part_f[:, f], AX.X, op).then_inc(s_prep, 1)
            assert chain.v + 4 == PREP_ROWS
            for a in range(6):
                dve.wait_ge(s_prep_pe, EB * (a + 1) + (4 if a > 3 else 0))
                dve.tensor_copy(col[:, a, :], ps[:, a % 4, :]).then_inc(s_prep, 1)
            dve.wait_ge(s_prep, PREP_ROWS + 6)
            w16 = ring[:, 0:NCOL]
            chain.v = PREP_ROWS + 6
            chain(dve.tensor_copy(w16, col[:, C_W0, :]))
            chain(dve.tensor_tensor(col[:, C_W1, :], col[:, C_W0, :], w16, ALU.subtract))
            chain(dve.tensor_copy(col[:, C_W0, :], w16))
            chain(dve.tensor_copy(w16, col[:, C_W1, :]))
            chain(dve.tensor_tensor(col[:, C_W2, :], col[:, C_W1, :], w16, ALU.subtract))
            chain(dve.tensor_copy(col[:, C_W1, :], w16))
            chain(dve.tensor_copy(w16, col[:, C_W2, :]))
            chain(dve.tensor_copy(col[:, C_W2, :], w16))
            for pair in range(2):
                hi_row, lo_row = ps[0:1, 4 + 2 * pair, 0:ET], ps[0:1, 5 + 2 * pair, 0:ET]
                big = scan[0:1, 0, 0:ET]
                low = scan[0:1, 1, 0:ET]
                chain(dve.tensor_copy(big, hi_row))
                chain(dve.tensor_copy(low, lo_row))
                chain(dve.tensor_tensor_scan(big, big, big, -1.0, ALU.max, ALU.max))
                chain(dve.tensor_tensor_scan(low[:, ::-1], low[:, ::-1], low[:, ::-1], 1e6, ALU.min, ALU.min))
                dve.wait_ge(s_prep_pe, 29 + pair)
                for nb in range(2 if pair == 0 else 1):
                    if nb == 0:
                        assert chain.v == PREP_SCAN + 18 * pair
                    t = 4 * (nb + 2 * pair)
                    scratch = count_scratch
                    chain(dve.tensor_scalar(scratch, ps[:, 0, 0:ET], nidx[:, nb:nb + 1], None, ALU.is_lt))
                    chain(dve.tensor_reduce(tab_f[:, t:t + 1], scratch, AX.X, ALU.add))
                    chain(dve.tensor_scalar(scratch, ps[:, 1, 0:ET], nidx[:, nb:nb + 1], None, ALU.is_le))
                    chain(dve.tensor_reduce(tab_f[:, t + 1:t + 2], scratch, AX.X, ALU.add))
                    chain(dve.tensor_scalar(tab_f[:, t:t + 1], tab_f[:, t:t + 1], float(ET - 1), None, ALU.min))
                    chain(dve.scalar_tensor_tensor(out=tab_f[:, t + 1:t + 2], in0=tab_f[:, t:t + 1], scalar=1.0,
                                                   in1=tab_f[:, t + 1:t + 2], op0=ALU.add, op1=ALU.max))
                    chain(dve.scalar_tensor_tensor(out=tab_f[:, t + 2:t + 3], in0=tab_f[:, t:t + 1], scalar=512.0,
                                                   in1=tab_f[:, t + 1:t + 2], op0=ALU.mult, op1=ALU.add))
            dve.wait_ge(s_prep_pe, 31)
            chain(dve.tensor_copy(tab[0:1, :], ps[0:1, 2, 0:3 * P]))
            assert chain.v == PREP_STEPS

            def rest(n, par, v, use):
                wait(dve, s_e0, v)
                wait(dve, s_e12, v - 1 + CR)
                t0, ep = use
                dve.tensor_tensor(raw_rest[:, 0:n, :], raw[par][:, 0:n, :], ep, ALU.subtract).then_inc(s_erest, 1)

            def ep0(t0, n):
                return span(EP, t0 * EPW, n * EPW).rearrange("p (t k f) -> p t k f", k=3, f=DE)[:, :, 0, :]
            with dve.Fori(0, ET // EBLK // 2) as j:
                for c in range(2):
                    rest(EBLK, c, j * 2 + c + 1, (0, ep0((j * 2 + c) * EBLK, EBLK)))
            rest(ET % EBLK, 0, ET // EBLK + 1, (0, ep0(ET // EBLK * EBLK, ET % EBLK)))

            step = dve.alloc_register("onehot_step")
            dve.reg_mov(step, 0)

            def onehots(i_tab, offset, offset_w, edges_only):
                lo, hi = edge_range(dve, i_tab)
                with dve.Fori(lo, hi) as t:
                    k = dve.snap(step, min_val=0, max_val=1 << 20)
                    slot = dve.snap((k & (RING - 1)) * SETW, min_val=0, max_val=(RING - 1) * SETW)
                    wait(dve, s_used, k + 1)
                    if edges_only:
                        dve.tensor_scalar(span(ring, slot, P), iota1[:, 0:P], offset, one(col[:, C_DST, :], t),
                                          ALU.add, ALU.is_equal).then_inc(s_onehot, 1)
                    else:
                        def hot(at, width, *how):
                            return dve.tensor_scalar(span(ring, slot + at, width), iota1[:, 0:width], *how)
                        hot(0, GW, offset, one(col[:, C_KEY, :], t), ALU.add, ALU.is_equal)
                        hot(GW, GW, one(col[:, C_REM, :], t), None, ALU.is_equal)
                        hot(2 * GW, P, one(col[:, C_SRC, :], t), None, ALU.is_equal)
                        rel = dve.snap(k & (RING - 1), min_val=0, max_val=RING - 1)
                        drained(dve)(dve.tensor_tensor(one(keyrel, rel), one(col[:, C_KEYW, :], t), offset_w,
                                                       ALU.subtract))
                        for a, c in enumerate((C_W0, C_W1, C_W2)):
                            ins = hot(2 * GW + (a + 1) * P, P, one(keyrel, rel), one(col[:, c, :], t), ALU.is_equal,
                                      ALU.mult)
                        ins.then_inc(s_onehot, 1)
                    dve.reg_add(step, step, 1)

            with dve.Fori(0, NT) as c:
                onehots(c + T_CHUNK, one(off_c, c), None, True)

            chain = drained(dve)
            dve.sem_inc(s_zD, CR)
            dve.sem_inc(s_aggfree, CR)

            def norm(rows_, into, eps, k, free=None):
                chain(dve.bn_stats(bn, rows_))
                chain(dve.bn_aggr(mv, bn))
                dve.tensor_scalar(ve, mv[:, 1:2], eps, None, ALU.add).then_inc(s_var, 1)
                wait(dve, s_std, k + 1)
                chain(dve.reciprocal(rs, sd))
                if free:
                    free()
                return dve.tensor_scalar(into, rows_, mv[:, 0:1], rs, ALU.subtract, ALU.mult)

            def hrow_free(g):
                wait(dve, s_tp, g - 1 + CR)

            def z_rest(n, g, par, zo, source=None):
                wait(dve, s_z0, g + 1 + CR)
                wait(dve, s_z2, g - 1 + CR)
                return dve.tensor_tensor(resid[par], mmo[par][:, 0:D], span(Z[zo], n * ZW, D), ALU.subtract)

            def agg_read(q):
                wait(dve, s_agg, q + 1 + CR)

            def agg_done():
                dve.sem_inc(s_aggfree, 1)

            def sage_post(n, g, par, zo, b):
                wait(dve, s_mm, g + 1 + CR)
                z_rest(n, g, par, zo)
                dve.tensor_tensor(node(R_, n), mmo[par][:, D:2 * D], b_early[:, b, :], ALU.add).then_inc(s_zD, 1)

            def row_phase(phase, pre, post):
                g0 = NT * phase
                pre(0, g0, g0 % 2)

                def body(n, g, h, par):
                    pre(n, g, par)
                    post(n - 1, g - 1, 1 - par)
                tiles(dve, phase, body, first=1)
                post(NT - 1, g0 + NT - 1, (g0 + NT - 1) % 2)

            dve.wait_ge(s_x, 32)
            dve.wait_ge(s_w, 16 * 16)

            def pre_first(n, g, par):
                norm(node(X, n), hrow[par], LN_EPS, n, lambda: hrow_free(g)).then_inc(s_row, 1)
            row_phase(PH_PRE, pre_first, lambda n, g, par: sage_post(n, g, par, 0, 0))

            with dve.Fori(0, NG) as i:
                onehots(i, one(off_g, i), one(off_c, i), False)

            def pre_sage1(n, g, par):
                agg_read(g - NT)
                hrow_free(g)
                a = agg[1 - par]
                chain(dve.tensor_scalar(one(rdeg, n), a[:, D:D + 1], 1.0, None, ALU.max))
                chain(dve.reciprocal(one(rdeg, n), one(rdeg, n)))
                chain(dve.scalar_tensor_tensor(out=hrow[par], in0=a[:, 0:D], scalar=one(rdeg, n),
                                               in1=node(R_, n), op0=ALU.mult, op1=ALU.add))
                dve.sem_inc(s_row, 1)
                agg_done()
            row_phase(PH_SAGE1, pre_sage1, lambda n, g, par: sage_post(n, g, par, 1, 1))

            def pre_sage2(n, g, par):
                agg_read(g - NT)
                hrow_free(g)
                chain(dve.scalar_tensor_tensor(out=urow, in0=agg[1 - par][:, 0:D], scalar=one(rdeg, n),
                                               in1=node(R_, n), op0=ALU.mult, op1=ALU.add))
                agg_done()
                chain(dve.tensor_tensor(node(X, n), node(X, n), urow, ALU.add))
                norm(node(X, n), hrow[par], LN_EPS, n + NT).then_inc(s_row, 1)

            def post_sage2(n, g, par):
                wait(dve, s_z0, g + 1 + CR)
                dve.sem_inc(s_zD, 1)
            row_phase(PH_SAGE2, pre_sage2, post_sage2)

            dve.wait_ge(s_wlate, 16 * 11)

            def pre_gcn(n, g, par):
                agg_read(g - NT)
                hrow_free(g)
                chain(dve.tensor_tensor(urow, agg[1 - par][:, 0:D], late["b_gcn"], ALU.add))
                agg_done()
                chain(dve.tensor_tensor(node(X, n), node(X, n), urow, ALU.add))
                chain(norm(node(X, n), urow, LN_EPS, n + 2 * NT))
                dve.tensor_scalar(node(R_, n), urow, 0.0, None, ALU.max)
                dve.tensor_copy(hrow[par], urow).then_inc(s_row, 1)

            def post_gcn(n, g, par):
                wait(dve, s_mm, g + 1 + CR)
                z_rest(n, g, par, 1).then_inc(s_zD, 1)
            row_phase(PH_GCN, pre_gcn, post_gcn)

            g0, ln0 = NT * PH_INTER, 3 * NT

            def inner(n, g, par, ln):
                agg_read(g - NT)
                chain(dve.scalar_tensor_tensor(out=urow, in0=agg[1 - par][:, 0:D], scalar=0.0, in1=node(R_, n),
                                               op0=ALU.max, op1=ALU.add))
                agg_done()
                wait(dve, s_tv, n)
                chain(norm(urow, inner_row, LN_EPS_INTER, ln).then_inc(s_inner, 1))

            def outer(n, g, par, ln):
                wait(dve, s_tb, n + 1)
                chain(dve.tensor_tensor(urow, tb, node(R_, n), ALU.add))
                chain(norm(urow, urow, LN_EPS_INTER, ln))
                chain(dve.tensor_tensor(urow, urow, late["s_out"], ALU.mult))
                chain(dve.tensor_tensor(urow, urow, late["b_out"], ALU.add))
                chain(dve.tensor_tensor(node(X, n), node(X, n), urow, ALU.add))
                norm(node(X, n), hrow[par], LN_EPS, ln + 1, lambda: hrow_free(g)).then_inc(s_row, 1)

            def topk(n, g, par):
                wait(dve, s_mm, g + 1 + CR)
                wait(dve, s_z2, g - 1 + CR)
                chain(dve.tensor_copy(keep, mmo[par][:, 0:D]))
                from_ = keep
                for r in range(TOPK // 8):
                    chain(dve.max(out=mx8, in_=from_))
                    chain(dve.match_replace(out=urow, in_to_replace=mx8, in_values=from_, imm_value=LOWEST))
                    from_ = urow
                chain(dve.tensor_tensor(urow, urow, keep, ALU.not_equal))
                chain(dve.tensor_tensor(resid[par], keep, urow, ALU.mult))
                chain(dve.tensor_copy(span(Z[0], n * ZW, D), resid[par]))
                dve.tensor_copy(node(R_, n), mmo[par][:, D:2 * D])
                dve.tensor_tensor(resid[par], resid[par], span(Z[0], n * ZW, D), ALU.subtract).then_inc(s_zD, 1)


            def inter(n, g, par, ln, do):
                k = ln
                for what in "iok":
                    if what not in do:
                        continue
                    if what == "i":
                        inner(n, g, par, k)
                        k = k + 1
                    elif what == "o":
                        outer(n - 1, g - 1, 1 - par, k)
                        k = k + 2
                    else:
                        topk(n - 2, g - 2, par)
            inter(0, g0, g0 % 2, ln0, "i")
            inter(1, g0 + 1, (g0 + 1) % 2, ln0 + 1, "io")
            with dve.Fori(0, (NT - 3) // 2) as j:
                for c in range(2):
                    inter(j * 2 + (2 + c), j * 2 + (g0 + 2 + c), (g0 + c) % 2,
                          j * 6 + (ln0 + 4 + 3 * c), "iok")
            inter(NT - 1, g0 + NT - 1, (g0 + NT - 1) % 2, ln0 + 3 * NT - 5, "iok")
            inter(NT, g0 + NT, (g0 + NT) % 2, ln0 + 3 * NT - 2, "ok")
            inter(NT + 1, g0 + NT + 1, (g0 + NT + 1) % 2, None, "k")

            def last(n, g, h, par):
                agg_read(g - NT)
                chain(dve.scalar_tensor_tensor(out=urow, in0=agg[1 - par][:, 0:D], scalar=one(rdeg, n),
                                               in1=node(R_, n), op0=ALU.mult, op1=ALU.add))
                agg_done()
                chain(dve.tensor_tensor(node(X, n), node(X, n), urow, ALU.add).then_inc(s_done, 1))
            tiles(dve, PH_MAXK, last)

        @block.tensor
        def _(pe):
            pe.sem_inc(s_used, RING)
            pe.sem_inc(s_tp, CR)
            pe.sem_inc(s_mm, CR)
            pe.sem_inc(s_agg, CR)
            pe.wait_ge(s_const, 7)
            pe.wait_ge(s_prep, PREP_ROWS)

            def transpose_rows_of(a, from_):
                for c in range(EB):
                    pe.transpose(ps[:, a % 4, c * P:(c + 1) * P], from_[:, c, :], ident[:, :]).then_inc(s_prep_pe, 1)
            for a, from_ in enumerate((part_f[:, 0], part_f[:, 1], part_f[:, 2], rows[:, 2])):
                transpose_rows_of(a, from_)
            for a in range(4):
                for c in range(EB):
                    m = pe.matmul(ps[0:1, 4 + a, c * P:(c + 1) * P], stat[:, a, c:c + 1], ident[:, :],
                                  start=True, stop=True, skip_group_check=True)
                m.then_inc(s_prep_pe, 1)
            for a, from_ in ((4, part_f[:, 8]), (5, part_f[:, 7])):
                pe.wait_ge(s_prep, PREP_ROWS + a - 3)
                transpose_rows_of(a, from_)
            pe.wait_ge(s_prep, PREP_SCAN)
            for k in range(2):
                m = pe.matmul(ps[:, k, 0:ET], ones_row[0:1, :], scan[0:1, k, 0:ET], start=True, stop=True)
            m.then_inc(s_prep_pe, 1)
            pe.wait_ge(s_prep, PREP_SCAN + 14 + 4)
            for k in range(2):
                m = pe.matmul(ps[:, k, 0:ET], ones_row[0:1, :], scan[0:1, k, 0:ET], start=True, stop=True)
            m.then_inc(s_prep_pe, 1)
            pe.wait_ge(s_prep, PREP_STEPS - 1)
            for k, t in enumerate((2, 6, 10)):
                m = pe.matmul(ps[0:1, 2, k * P:(k + 1) * P], tab_f[:, t:t + 1], ident[:, :], start=True, stop=True,
                              skip_group_check=True)
            m.then_inc(s_prep_pe, 1)
            pe.wait_ge(s_prep, PREP_STEPS)

            step = pe.alloc_register("set_step")
            pe.reg_mov(step, 0)

            def clear(bank, at):
                return pe.matmul(bank[:, at:at + 1], zeros[:, :], zeros[:, 0:1], start=True, stop=True,
                                 skip_group_check=True)

            def accumulate(i_tab, banks, edges_only):
                lo, hi = edge_range(pe, i_tab)
                for b in banks:
                    clear(b, 500)
                with pe.Fori(lo, hi) as t:
                    k = pe.snap(step, min_val=0, max_val=1 << 20)
                    slot = pe.snap((k & (RING - 1)) * SETW, min_val=0, max_val=(RING - 1) * SETW)
                    wait(pe, s_onehot, k + 1)
                    if edges_only:
                        m = pe.matmul(banks[0][:, 0:EPW], span(ring, slot, P), span(EP, t * EPW, EPW),
                                      start=False, stop=True, skip_group_check=True)
                    else:
                        for a, (bank, at) in enumerate(((banks[0], 0), (banks[1], GW), (banks[1], GW), (banks[1], GW))):
                            m = pe.matmul(bank[:, 0:GW], span(ring, slot + (2 * GW + a * P), P),
                                          span(ring, slot + at, GW), start=False, stop=True, skip_group_check=True)
                    m.then_inc(s_used, 1)
                    pe.reg_add(step, step, 1)
                pe.matmul(banks[0][:, 501:502], zeros[:, :], zeros[:, 0:1], start=False, stop=True,
                          skip_group_check=True).then_inc(s_built, 1)

            pe.wait_ge(s_e12, -(-ET // EBLK) + CR)

            def edge_chunk(c, g, h, par):
                wait(pe, s_ea, c - 1 + CR)
                accumulate(c + T_CHUNK, [cnt_ps[par]], True)
            tiles(pe, 0, edge_chunk)

            def transpose_rows(g, par):
                wait(pe, s_row, g + 1)
                wait(pe, s_hT, g - 1 + CR)
                for k in range(2):
                    m = pe.transpose(tp[par][:, k * P:(k + 1) * P], hrow[par][:, k * P:(k + 1) * P], ident[:, :])
                m.then_inc(s_tp, 1)

            def multiply(g, par, W):
                wait(pe, s_hT, g + 1 + CR)
                wait(pe, s_z0, g - 1 + CR)
                wait(pe, s_zD, g - 1 + CR)
                width = W.shape[2]
                for k in range(2):
                    m = pe.matmul(mmo[par][:, 0:width], hT[par][:, k * P:(k + 1) * P], W[:, k, :],
                                  start=(k == 0), stop=(k == 1))
                m.then_inc(s_mm, 1)

            pe.wait_ge(s_w, 16 * 16)

            def pre(n, g, h, par):
                transpose_rows(g, par)
                multiply(g, par, W_early[:, 0])
            tiles(pe, PH_PRE, pre)

            pe.wait_ge(s_hT, NT + CR)
            pe.wait_ge(s_ea, NT + CR)

            with pe.Fori(0, NT) as c:
                for t in range(PER):
                    wait(pe, s_taken, c * PER + (t - 1 + CR))
                    accumulate(pe.snap(c * PER + t, min_val=0, max_val=NG - 1), [cnt_ps[t % 2], wgt_ps[t % 2]], False)
            pe.wait_ge(s_taken, NG + CR)

            def aggregate(i, n, q, h, par, b0, b1):
                if b0 == 0:
                    wait(pe, s_blk[par], h * 16 + 16)
                    wait(pe, s_aggfree, q - 1 + CR)
                for b in range(b0, b1):
                    if i == 2:
                        m = pe.matmul(agg[par][:, 0:D], BLK32[par][:, b * P:(b + 1) * P],
                                      ZFULL[0][:, b * D:(b + 1) * D], start=(b == 0), stop=(b == NT - 1),
                                      skip_group_check=True)
                        continue
                    for part in (2, 1, 0):
                        wide = D + 1 if i == 0 and part == 2 else D
                        m = pe.matmul(agg[par][:, 0:wide], BLK16[par][:, b * P:(b + 1) * P],
                                      Z[zin(i)][:, b * ZW + part * D:b * ZW + part * D + wide],
                                      start=(b == 0 and part == 2), stop=(b == NT - 1 and part == 0),
                                      skip_group_check=True)
                if b1 == NT:
                    m.then_inc(s_agg, 1)

            def z_ready(phase):
                for s in (s_z0, s_zD, s_z2):
                    pe.wait_ge(s, NT * (phase + 1) + CR)

            def row_layer(i, W):
                phase = i + 1
                z_ready(i)
                q0, g0 = NT * i, NT * phase
                aggregate(i, 0, q0, q0 // 2, q0 % 2, 0, NT)

                def body(n, q, h, par):
                    aggregate(i, n, q, h, par, 0, 12)
                    transpose_rows(q + (NT - 1), par)
                    aggregate(i, n, q, h, par, 12, 18)
                    multiply(q + (NT - 1), par, W)
                    aggregate(i, n, q, h, par, 18, NT)
                tiles(pe, i, body, first=1)
                g = g0 + NT - 1
                transpose_rows(g, g % 2)
                multiply(g, g % 2, W)

            row_layer(0, W_early[:, 1])
            pe.wait_ge(s_wlate, 16 * 11)
            row_layer(1, wk(late["W_gcn"], D))
            row_layer(2, wk(late["W_msg"], D))

            i = 3
            z_ready(i)
            q0, g0 = NT * i, NT * PH_INTER
            maxk_w = wk(late["W_maxk"], 2 * D)

            def edges_in(n):
                wait(pe, s_ean, n * 16 + 16)
                pe.transpose(mlp_ps[:, 0:P], ea_now[:, :], ident[:, :]).then_inc(s_eat, 1)

            def edges_add(n, par):
                wait(pe, s_eac, n + 1)
                pe.matmul(agg[par][:, 0:D], eaT[:, :], late["W_edge"][0:DE, :], start=False, stop=False,
                          skip_group_check=True)

            def inner_transpose(n):
                wait(pe, s_inner, n + 1)
                for k in range(2):
                    m = pe.transpose(tv[:, k * P:(k + 1) * P], inner_row[:, k * P:(k + 1) * P], ident[:, :])
                m.then_inc(s_tv, 1)

            def mlp_layer(n, l):
                if l == 0:
                    wait(pe, s_g0, n + 1)
                else:
                    wait(pe, s_g, n * 3 + l)
                W = wk(late[f"mlp{l}"], D)
                for o in range(2):
                    for k in range(2):
                        m = pe.matmul(mlp_ps[:, o * P:(o + 1) * P], W[:, k, o * P:(o + 1) * P],
                                      GT[:, l % 2, k * P:(k + 1) * P], start=(k == 0), stop=(k == 1))
                m.then_inc(s_q, 1)

            def back(n):
                wait(pe, s_g, n * 3 + 3)
                for k in range(2):
                    m = pe.transpose(tb[:, k * P:(k + 1) * P], GT[:, 1, k * P:(k + 1) * P], ident[:, :])
                m.then_inc(s_tb, 1)

            def inter(n, q, h, par, here=True, back1=True, back2=True):
                cuts = [0, 3, 6, 8, 12, 16, 20, NT]
                steps = [lambda: edges_in(n) if here else None,
                         lambda: (edges_add(n, par) if here else None,
                                  transpose_rows(q + (NT - 2), 1 - par) if back2 else None),
                         lambda: inner_transpose(n - 1) if back1 else None,
                         lambda: (multiply(q + (NT - 2), 1 - par, maxk_w) if back2 else None,
                                  mlp_layer(n - 1, 0) if back1 else None),
                         lambda: mlp_layer(n - 1, 1) if back1 else None,
                         lambda: mlp_layer(n - 1, 2) if back1 else None,
                         lambda: back(n - 1) if back1 else None]
                for s, f in enumerate(steps):
                    if here:
                        aggregate(i, n, q, h, par, cuts[s], cuts[s + 1])
                    f()

            inter(0, q0, q0 // 2, q0 % 2, back1=False, back2=False)
            inter(1, q0 + 1, (q0 + 1) // 2, (q0 + 1) % 2, back2=False)
            with pe.Fori(0, (NT - 3) // 2) as j:
                for c in range(2):
                    inter(j * 2 + (2 + c), j * 2 + (q0 + 2 + c), j + (q0 + 2 + c) // 2, (q0 + c) % 2)
            q = q0 + NT - 1
            inter(NT - 1, q, q // 2, q % 2)
            inter(NT, q + 1, None, (q + 1) % 2, here=False)
            inter(NT + 1, q + 2, None, (q + 2) % 2, here=False, back1=False)

            z_ready(4)
            tiles(pe, 4, lambda n, q, h, par: aggregate(4, n, q, h, par, 0, NT))




_WEIGHTS = ["L0_gnn_W_l1", "L0_gnn_b1", "L0_gnn_W_r1", "L0_gnn_W_l2", "L0_gnn_b2", "L0_gnn_W_r2", "L1_gnn_W",
            "L1_gnn_b", "L2_gnn_W_message", "L2_gnn_mlp_W0", "L2_gnn_mlp_b0", "L2_gnn_mlp_W1", "L2_gnn_mlp_b1",
            "L2_gnn_mlp_W2", "L2_gnn_mlp_b2", "L2_gnn_ln_aggr_scale", "L2_gnn_ln_aggr_bias", "L2_gnn_ln_out_scale",
            "L2_gnn_ln_out_bias", "L3_gnn_W_self", "L3_gnn_W_neigh"]
_INPUTS = ["x", "src", "dst", "edge_attr_64", "edge_weight"] + _WEIGHTS


def kernel(**inputs):
    import concourse.bacc as bacc
    from concourse.bass_utils import run_bass_kernel_spmd as run

    nc = bacc.Bacc("TRN2", target_bir_lowering=False, num_devices=1)
    arrays, aps = {}, {}
    for name in _INPUTS:
        arrays["in_" + name] = np.ascontiguousarray(inputs[name])
        a = arrays["in_" + name]
        aps[name] = nc.dram_tensor("in_" + name, a.shape, mybir.dt.from_np(a.dtype), kind="ExternalInput").ap()
    out = nc.dram_tensor("out_0", (N, D), F32, kind="ExternalOutput").ap()
    build(nc, aps["x"], aps["src"], aps["dst"], aps["edge_attr_64"], aps["edge_weight"],
          {k: aps[k] for k in _WEIGHTS}, out)
    return run(nc, [arrays], core_ids=[0]).results[0]["out_0"]
```

```python
from contextlib import ExitStack

import numpy as np
import concourse.bass as bass
from concourse import mybir
from concourse.alu_op_type import AluOpType as ALU

F32, F16, BF16, I32 = mybir.dt.float32, mybir.dt.float16, mybir.dt.bfloat16, mybir.dt.int32
ACT = mybir.ActivationFunctionType
AX = mybir.AxisListType

P = 128
N, D, E, DE = 3125, 256, 50000, 64
NT = -(-N // P)
NR = N - (NT - 1) * P
ET = -(-E // P)
ER = E - (ET - 1) * P
EB = -(-ET // P)
G = 16
PER = P // G
NG = NT * PER
GW = NT * G
SG = P // G
TOPK = 32
PAD_DST = 4095
ZW = 3 * D + 2
RING = 3
O_P, O_Q, O_R, O_S, O_SW = 0, GW, 2 * GW, 2 * GW + P, 2 * GW + 2 * P
SETW = 2 * GW + 5 * P
RT = ET + RING - 1
RLOADS = 6
NPAIR = NT // 2
CR = 2
PH_PRE, PH_SAGE1, PH_SAGE2, PH_GCN, PH_INTER, PH_MAXK = range(6)
LN_EPS, LN_EPS_INTER = 1e-5, 1e-6
LOWEST = -3.4e38
PREP_ROWS = 12 + (SG - 2) + 5 + 2
PREP_SCAN = PREP_ROWS + 6 + 8 + 4
PREP_STEPS = PREP_SCAN + 14 + 1
PE_EXTREMES = 4 * EB + 2
PE_TABLES = PE_EXTREMES + 2 * EB


def build(nc, x, src, dst, edge_attr, edge_weight, w, out):
    ctx = ExitStack()
    with ctx:
        def sb(name, shape, dt):
            return ctx.enter_context(nc.sbuf_tensor(name, shape, dt))

        def sem(name):
            return ctx.enter_context(nc.semaphore(name))

        cnt_dram = nc.dram_tensor("cnt_blocks", (NT, P, NT * P), F16, kind="Internal").ap()
        wgt_dram = nc.dram_tensor("wgt_blocks", (NT * P, NT * P), F32, kind="Internal").ap()
        ea_dram = nc.dram_tensor("edge_sums", (NT * P, DE), F32, kind="Internal").ap()

        XW, ZF = NT * D, NT * ZW // 2
        BLKF = NT * P
        arena = sb("arena", [P, 2 * XW + 2 * ZF + 2 * BLKF], F32)

        def region(at, words):
            return arena[:, at:at + words]

        o_r, o_z0, o_z1, o_blk = XW, 2 * XW, 2 * XW + ZF, 2 * XW + 2 * ZF
        X = region(0, XW).rearrange("p (n d) -> p n d", d=D)
        R_ = region(o_r, XW).rearrange("p (n d) -> p n d", d=D)
        Z = [region(o, ZF).bitcast(BF16) for o in (o_z0, o_z1)]
        ZFULL = [region(o, XW) for o in (o_z0, o_z1)]
        BLK32 = [region(o_blk + b * BLKF, BLKF) for b in range(2)]
        BLK16 = [region(o_blk + b * BLKF, BLKF // 2).bitcast(F16) for b in range(2)]
        rows = region(0, 3 * EB * P).rearrange("p (a c e) -> p a c e", a=3, c=EB)
        rows_i = rows.bitcast(I32)
        ROW0 = 3 * EB * P
        part_i = region(ROW0, 3 * EB * P).bitcast(I32).rearrange("p (a c e) -> p a c e", a=3, c=EB)
        part_f = region(2 * ROW0, 9 * EB * P).rearrange("p (a c e) -> p a c e", a=9, c=EB)
        o_raw = 2 * ROW0 + 9 * EB * P
        raw = region(o_raw, RT * DE).rearrange("p (t f) -> p t f", f=DE)
        o_sc, o_se = o_raw + RT * DE, o_raw + RT * DE + BLKF
        stage_w = [region(b * BLKF, BLKF).rearrange("p (t s) -> p t s", s=GW) for b in range(2)]
        stage_c = [region(o_sc + b * BLKF // 2, BLKF // 2).bitcast(F16).rearrange("p (b d) -> p b d", d=P)
                   for b in range(2)]
        stage_e = [arena[0:G, o_se + b * PER * DE:o_se + (b + 1) * PER * DE].rearrange("p (t f) -> p t f", f=DE)
                   for b in range(2)]

        NCOL = EB * P
        front = sb("front", [P, 8 * NCOL + RING * SETW // 2], F32)
        col = front[:, 0:8 * NCOL].rearrange("p (a t) -> p a t", a=8)
        C_P, C_T, C_R, C_W0, C_S, C_Q, C_W1, C_W2 = range(8)
        ring = front[:, 8 * NCOL:].bitcast(BF16)
        late = {}
        at = 0
        for name, width in (("W_gcn", 2 * D), ("W_msg", 2 * D), ("W_maxk", 4 * D), ("mlp0", 2 * D), ("mlp1", 2 * D),
                            ("mlp2", 2 * D), ("W_edge", D), ("b_gcn", D), ("s_out", D), ("b_out", D)):
            late[name] = front[:, at:at + width]
            at += width

        def wk(ap, n):
            return ap.rearrange("p (k n) -> p k n", n=n)

        W_early = sb("W_early", [P, 2, 2, 2 * D], F32)
        b_early = sb("b_early", [P, 2, D], F32)
        mlp_col = sb("mlp_col", [P, 5, 2], F32)
        ident = sb("ident", [P, P], F32)
        iota1 = sb("iota1", [P, GW], F16)
        off_g = sb("off_g", [P, NG], F32)
        off_t = sb("off_t", [P, NG], F32)
        r_s_col = sb("r_s_col", [P, 2, RING], F32)
        hot_t = sb("hot_t", [P, RING, G], F32)
        nidx = sb("nidx", [P, 2], F32)
        zeros = sb("zeros", [P, P], BF16)
        ones_row = sb("ones_row", [1, P], F32)
        work = sb("work", [P, 12, D], F32)
        hrow = [work[:, b, :] for b in range(2)]
        hT = [work[:, 2 + b, :] for b in range(2)]
        resid = [work[:, 4 + b, :] for b in range(2)]
        GT = work[:, 6:8, :]
        YT = work[:, 8, :]
        urow = work[:, 9, :]
        inner_row, keep = work[:, 10, :], work[:, 11, :]
        count_scratch = work[:, 8:10, :].rearrange("p a d -> p (a d)")[:, 0:ET]
        small = sb("small", [P, 32], F32)
        bn, mv, ve, sd, rs, mx8 = (small[:, 0:6], small[:, 6:8], small[:, 8:9], small[:, 9:10], small[:, 10:11],
                                   small[:, 16:24])
        rdeg = sb("rdeg", [P, NT], F32)
        stat = sb("stat", [P, 2, EB], F32)
        scan = work[0:1, 4:8, :].rearrange("o (a b) d -> o a (b d)", a=2)
        tab_f = sb("tab_f", [P, 8], F32)
        tab = sb("tab", [1, 2 * P], I32)
        ea_now = sb("ea_now", [P, P], F32)
        eaT = sb("eaT", [DE, P], F32)

        ps = ctx.enter_context(nc.psum_tensor("ps", [P, 8, 512], F32))
        agg = [ps[:, b, :] for b in range(2)]
        tp = [ps[:, 2 + b, 0:D] for b in range(2)]
        mmo = [ps[:, 4 + b, :] for b in range(2)]
        mlp_ps = ps[:, 6, 0:D]
        tv, tb = ps[:, 7, 0:D], ps[:, 7, D:2 * D]
        cnt_ps = [ps[:, b, :] for b in range(2)]
        wgt_ps = [ps[:, 2 + b, :] for b in range(2)]

        s_const = sem("constants_ready")
        s_rows = sem("edge_rows_loaded")
        s_pad = sem("padding_set")
        s_prep = sem("dve_prep_step")
        s_prep_pe = sem("pe_prep_step")
        s_raw = sem("edge_features_loaded")
        s_hotD = sem("p_q_t_ready")
        s_hotP = sem("r_s_ready")
        s_hotA = sem("weighted_s_ready")
        s_made = sem("sets_begun_by_pool")
        s_used = sem("onehots_used")
        s_built = sem("tile_built")
        s_taken = sem("built_tile_taken")
        s_store_c = [sem(f"count_block_stored{b}") for b in range(2)]
        s_store_w = [sem(f"weight_block_stored{b}") for b in range(2)]
        s_store_e = [sem(f"edge_sums_stored{b}") for b in range(2)]
        s_w = sem("early_weights_loaded")
        s_wlate = sem("late_weights_loaded")
        s_x = sem("x_loaded")
        s_xpad = sem("x_padding_set")
        s_blk = [sem(f"block_loaded{b}") for b in range(2)]
        s_agg = sem("aggregated")
        s_aggfree = sem("aggregate_read")
        s_var = sem("variance_ready")
        s_std = sem("deviation_ready")
        s_row = sem("rows_normalised")
        s_tp = sem("rows_transposed")
        s_hT = sem("transpose_copied")
        s_mm = sem("rows_multiplied")
        s_z0 = sem("first_part_ready")
        s_zD = sem("rest_ready")
        s_z2 = sem("parts_ready")
        s_inner = sem("inner_norm_ready")
        s_tv = sem("inner_rows_transposed")
        s_g0 = sem("inner_rows_copied")
        s_q = sem("mlp_layer_multiplied")
        s_y = sem("mlp_layer_activated")
        s_g = sem("mlp_layer_added")
        s_tb = sem("mlp_rows_back")
        s_ean = sem("edge_sums_at_hand")
        s_eat = sem("edge_sums_transposed")
        s_eac = sem("edge_transpose_copied")
        s_done = sem("rows_final")
        s_out = sem("output_stored")

        block = ctx.enter_context(nc.Block())

        def wait(e, s, v):
            e.wait_ge(s, v if isinstance(v, int) else e.snap(v))

        class Chain:

            def __init__(self, e, s):
                self.e, self.s, self.v = e, s, 0

            def __call__(self, ins):
                ins.then_inc(self.s, 1)
                self.v += 1
                self.e.wait_ge(self.s, self.v)

        def drained(e):
            def step(ins):
                e.drain()
            return step

        def tiles(e, phase, body, first=0):
            k0 = NT * phase + first
            with e.Fori(0, (NT - first) // 2) as j:
                for c in range(2):
                    body(j * 2 + (first + c), j * 2 + (k0 + c), j + (k0 + c) // 2, (k0 + c) % 2)
            if (NT - first) % 2:
                g = NT * phase + NT - 1
                body(NT - 1, g, g // 2, g % 2)

        def one(ap, n):
            return ap[:, n:n + 1] if isinstance(n, int) else ap[:, bass.ds(n, 1)]

        def span(ap, start, width):
            return ap[:, start:start + width] if isinstance(start, int) else ap[:, bass.ds(start, width)]

        def node(ap, n):
            return ap[:, n, :] if isinstance(n, int) else ap[:, bass.ds(n, 1), :].rearrange("p a d -> p (a d)")

        def bounded(v, low, high):
            return nc.s_assert_within(v, low, high, skip_runtime_bounds_check_because="the table is clamped to it")

        def zin(i):
            return i % 2

        def part_of(u, at, width):
            return ring[:, u * SETW + at:u * SETW + at + width]

        def walk(e, kind, c, per_edge_tile, after=None, before=None):
            _, packed = nc.values_load_multi_w_load_instructions(
                tab[0:1, c * PER:(c + 1) * PER] if isinstance(c, int) else tab[0:1, bass.ds(c * PER, PER)],
                engines=[kind], min_val=1, max_val=(ET - 1) * 512 + ET,
                skip_runtime_bounds_check_because="the table is clamped to it")
            for i in range(PER):
                lo = bounded(e.snap(packed[i] >> 9), 0, ET - 1)
                hi = bounded(e.snap(packed[i] & 511), 1, ET)
                if before:
                    before(i)
                with e.Fori(lo, hi, RING) as t:
                    k = e.snap(step_of[kind], min_val=0, max_val=1 << 20)
                    for u in range(RING):
                        per_edge_tile(k, u, t + u, i)
                    e.reg_add(step_of[kind], step_of[kind], RING)
                if after:
                    after(i)
        step_of = {}

        def start_walk(e, kind):
            step_of[kind] = e.alloc_register("sets")
            e.reg_mov(step_of[kind], 0)

        @block.sync
        def _(sp):
            sp.wait_ge(s_pad, 3)
            full = (E // P) // P * P
            for a, t in enumerate((src, dst, edge_weight)):
                into = rows_i if a < 2 else rows
                for c in range(EB - 1):
                    sp.dma_start(into[:, a, c, :], t[c * P * P:(c + 1) * P * P].rearrange("(p e) -> p e", e=P)
                                 ).then_inc(s_rows, 16)
                sp.dma_start(into[0:ET - 1 - full, a, EB - 1, :],
                             t[full * P:(ET - 1) * P].rearrange("(p e) -> p e", e=P)).then_inc(s_rows, 16)
                sp.dma_start(into[ET - 1 - full:ET - full, a, EB - 1, 0:ER],
                             t[(ET - 1) * P:E].rearrange("(p e) -> p e", p=1)).then_inc(s_rows, 16)
            for i, (l, r, b) in enumerate((("W_l1", "W_r1", "b1"), ("W_l2", "W_r2", "b2"))):
                for h, name in enumerate((l, r)):
                    sp.dma_start(W_early[:, i, :, h * D:(h + 1) * D],
                                 w["L0_gnn_" + name].rearrange("(k p) n -> p k n", p=P)).then_inc(s_w, 16)
                sp.dma_start(b_early[:, i, :], w["L0_gnn_" + b].rearrange("(o n) -> o n", o=1).broadcast_to([P, D])
                             ).then_inc(s_w, 16)
            for i, name in enumerate(("mlp_b0", "mlp_b1", "mlp_b2", "ln_aggr_scale", "ln_aggr_bias")):
                for k in range(2):
                    sp.dma_start(mlp_col[:, i, k:k + 1],
                                 w["L2_gnn_" + name][k * P:(k + 1) * P].rearrange("(p o) -> p o", o=1)
                                 ).then_inc(s_w, 16)

            def store(c, half, par):
                wait(sp, s_taken, c * PER + (PER + CR))
                dc = cnt_dram[c] if isinstance(c, int) else cnt_dram[bass.ds(c, 1)].rearrange("o p f -> (o p) f")
                rows_of = wgt_dram[bass.ds(c * P, P), :]
                sp.dma_start(dc, stage_c[par].rearrange("p b d -> p (b d)")).then_inc(s_store_c[par], 16)
                sp.dma_start(rows_of.rearrange("(t d) (g s) -> (d g) t s", d=G, g=SG), stage_w[par]
                             ).then_inc(s_store_w[par], 16)
                sp.dma_start(ea_dram[bass.ds(c * P, P), :].rearrange("(t d) f -> d t f", d=G), stage_e[par]
                             ).then_inc(s_store_e[par], 16)

            with sp.Fori(0, NPAIR) as j:
                for c in range(2):
                    store(j * 2 + c, j, c)
            store(NT - 1, NPAIR, 0)

            sp.wait_ge(s_built, NG)
            sp.wait_ge(s_xpad, 2)
            sp.dma_start(X[:, 0:NT - 1, :], x[0:(NT - 1) * P, :].rearrange("(n p) d -> p n d", p=P)).then_inc(s_x, 16)
            sp.dma_start(X[0:NR, NT - 1, :], x[(NT - 1) * P:N, :]).then_inc(s_x, 16)
            for name, of in (("W_gcn", "L1_gnn_W"), ("mlp0", "L2_gnn_mlp_W0"), ("mlp1", "L2_gnn_mlp_W1"),
                             ("mlp2", "L2_gnn_mlp_W2")):
                sp.dma_start(wk(late[name], D), w[of].rearrange("(k p) n -> p k n", p=P)).then_inc(s_wlate, 16)
            sp.dma_start(wk(late["W_msg"], D), w["L2_gnn_W_message"][0:D, :].rearrange("(k p) n -> p k n", p=P)
                         ).then_inc(s_wlate, 16)
            sp.dma_start(late["W_edge"][0:DE, :], w["L2_gnn_W_message"][D:D + DE, :]).then_inc(s_wlate, 16)
            for h, of in enumerate(("L3_gnn_W_neigh", "L3_gnn_W_self")):
                sp.dma_start(wk(late["W_maxk"], 2 * D)[:, :, h * D:(h + 1) * D],
                             w[of].rearrange("(k p) n -> p k n", p=P)).then_inc(s_wlate, 16)
            for name, of in (("b_gcn", "L1_gnn_b"), ("s_out", "L2_gnn_ln_out_scale"), ("b_out", "L2_gnn_ln_out_bias")):
                sp.dma_start(late[name], w[of].rearrange("(o n) -> o n", o=1).broadcast_to([P, D])
                             ).then_inc(s_wlate, 16)

            for par in range(2):
                uses = (NT + 1 - par) // 2
                sp.wait_ge(s_store_c[par], 16 * uses)
                sp.wait_ge(s_store_w[par], 16 * uses)
                sp.wait_ge(s_store_e[par], 16 * uses)
            for i in range(5):
                def load(n, q, h, par, i=i):
                    wait(sp, s_agg, q + 1)
                    if i == 2:
                        cols = wgt_dram[:, bass.ds(n * P, P)].rearrange("(b p) s -> p b s", p=P)
                        sp.dma_start(BLK32[par].rearrange("p (b s) -> p b s", s=P), cols).then_inc(s_blk[par], 16)
                    else:
                        f = cnt_dram[n] if isinstance(n, int) else \
                            cnt_dram[bass.ds(n, 1)].rearrange("o p f -> (o p) f")
                        sp.dma_start(BLK16[par], f).then_inc(s_blk[par], 16)
                    if i == 3:
                        wait(sp, s_eat, n)
                        sp.dma_start(ea_now[:, 0:DE], ea_dram[bass.ds(n * P, P), :]).then_inc(s_ean, 16)
                tiles(sp, i, load)

            def store_out(n, g, h, par):
                wait(sp, s_done, n + 1)
                sp.dma_start(out[bass.ds(n * P, P), :], node(X, n)).then_inc(s_out, 16)

            with sp.Fori(0, NT - 1) as n:
                store_out(n, 0, 0, 0)
            sp.wait_ge(s_done, NT)
            sp.dma_start(out[(NT - 1) * P:N, :], X[0:NR, NT - 1, :]).then_inc(s_out, 16)
            sp.wait_ge(s_out, 16 * NT)

        @block.gpsimd
        def _(pool):
            chain = drained(pool)
            pool.memset(rows_i[:, 0, EB - 1, :], 0).then_inc(s_pad, 1)
            pool.memset(rows_i[:, 1, EB - 1, :], PAD_DST).then_inc(s_pad, 1)
            pool.memset(rows[:, 2, EB - 1, :], 0.0).then_inc(s_pad, 1)
            pool.memset(raw[:, ET - 1:RT, :], 0.0).then_inc(s_pad, 1)
            chain(pool.memset(ident[:, :], 0.0))
            pool.affine_select(out=ident[:, :], in_=ident[:, :], compare_op=ALU.not_equal, fill=1.0, base=0,
                               pattern=[[-1, P]], channel_multiplier=1).then_inc(s_const, 1)
            pool.iota(iota1[:, :], pattern=[[1, GW]], base=1, channel_multiplier=0,
                      allow_small_or_imprecise_dtypes=True).then_inc(s_const, 1)
            pool.iota(off_g[:, :], pattern=[[GW, NG]], base=0, channel_multiplier=0,
                      allow_small_or_imprecise_dtypes=True).then_inc(s_const, 1)
            pool.iota(off_t[:, :], pattern=[[G, NG]], base=0, channel_multiplier=0,
                      allow_small_or_imprecise_dtypes=True).then_inc(s_const, 1)
            pool.iota(nidx[:, :], pattern=[[P, 2]], base=0, channel_multiplier=1,
                      allow_small_or_imprecise_dtypes=True).then_inc(s_const, 1)
            pool.memset(zeros[:, :], 0.0).then_inc(s_const, 1)
            pool.memset(ea_now[:, :], 0.0)
            pool.memset(ones_row[:, :], 1.0).then_inc(s_const, 1)
            pool.sem_inc(s_z2, CR)

            def r_and_s(k, u, t, i):
                if u == 0:
                    pool.drain()
                    chain(pool.tensor_copy(r_s_col[:, :, :], col[:, C_R:C_S + 1:C_S - C_R, bass.ds(t, RING)]))
                wait(pool, s_used, k + (u + 1))
                pool.sem_inc(s_made, 1)
                for c, at in ((1, O_S), (0, O_R)):
                    a = pool.tensor_scalar(part_of(u, at, P), iota1[:, 0:P], r_s_col[:, c, u:u + 1], None,
                                           ALU.is_equal)
                a.then_inc(s_hotP, 1)
            pool.wait_ge(s_prep, PREP_STEPS)
            start_walk(pool, mybir.EngineType.Pool)
            with pool.Fori(0, NT) as c:
                walk(pool, mybir.EngineType.Pool, c, r_and_s)

            pool.wait_ge(s_built, NG)
            for par in range(2):
                pool.wait_ge(s_store_w[par], 16 * ((NT + 1 - par) // 2))
            pool.memset(X[:, NT - 1, :], 0.0).then_inc(s_xpad, 1)
            pool.memset(Z[0].rearrange("p (n k) -> p n k", k=ZW)[:, :, 3 * D:ZW], 1.0).then_inc(s_xpad, 1)

            def split(n, g, h, par, zo):
                wait(pool, s_zD, g + 1 + CR)
                z1, z2 = (span(Z[zo], n * ZW + k * D, D) for k in (1, 2))
                chain(pool.tensor_copy(z1, resid[par]))
                pool.tensor_tensor(z2, resid[par], z1, ALU.subtract).then_inc(s_z2, 1)

            tiles(pool, PH_PRE, lambda n, g, h, par: split(n, g, h, par, 0))
            tiles(pool, PH_SAGE1, lambda n, g, h, par: split(n, g, h, par, 1))

            def none(n, g, h, par):
                wait(pool, s_zD, g + 1 + CR)
                pool.sem_inc(s_z2, 1)
            tiles(pool, PH_SAGE2, none)
            tiles(pool, PH_GCN, lambda n, g, h, par: split(n, g, h, par, 1))

            def mlp_sums(n):
                for l in range(3):
                    wait(pool, s_y, n * 3 + (l + 1))
                    pool.tensor_tensor(GT[:, (l + 1) % 2, :], GT[:, l % 2, :], YT, ALU.add).then_inc(s_g, 1)

            mlp_sums(0)
            mlp_sums(1)
            g0 = NT * PH_INTER

            with pool.Fori(0, NPAIR - 1) as j:
                for c in range(2):
                    split(j * 2 + c, j * 2 + (g0 + c), None, (g0 + c) % 2, 0)
                    mlp_sums(j * 2 + (c + 2))
            for n in range(2 * (NPAIR - 1), NT):
                split(n, g0 + n, None, (g0 + n) % 2, 0)
                if n + 2 < NT:
                    mlp_sums(n + 2)

        @block.scalar
        def _(act):
            act.sem_inc(s_hT, CR)
            act.sem_inc(s_z0, CR)
            act.sem_inc(s_taken, CR)

            per = -(-(ET - 1) // RLOADS)
            for t0 in range(0, ET - 1, per):
                t1 = min(t0 + per, ET - 1)
                act.dma_start(raw[:, t0:t1, :], edge_attr[t0 * P:t1 * P, :].rearrange("(t p) f -> p t f", p=P)
                              ).then_inc(s_raw, 16)
            act.wait_ge(s_pad, 4)
            act.dma_start(raw[0:ER, ET - 1, :], edge_attr[(ET - 1) * P:E, :]).then_inc(s_raw, 16)

            def take(c, par, t):
                wait(act, s_built, c * PER + (t + 1))
                act.activation(stage_c[par][:, :, t * G:(t + 1) * G],
                               cnt_ps[t % 2][:, 0:GW].rearrange("p (b d) -> p b d", d=G), ACT.Copy)
                act.activation(stage_e[par][:, t, :], cnt_ps[t % 2][0:G, GW:GW + DE], ACT.Copy)
                act.activation(stage_w[par][:, t, :], wgt_ps[t % 2][:, 0:GW], ACT.Copy).then_inc(s_taken, 1)

            def weigh(k, u, t, i):
                wait(act, s_hotP, k + (u + 1))
                for a, c in enumerate((C_W0, C_W1, C_W2)):
                    m = act.activation(part_of(u, O_SW + a * P, P), part_of(u, O_S, P), ACT.Copy,
                                       scale=one(col[:, c, :], t))
                m.then_inc(s_hotA, 1)

            def chunk(c, half, par):
                for s in (s_store_c, s_store_w, s_store_e):
                    wait(act, s[par], half * 16)
                walk(act, mybir.EngineType.Activation, c, weigh,
                     after=lambda t: take(c, par, t - 1) if t else None)
                take(c, par, PER - 1)
            act.wait_ge(s_prep, PREP_STEPS)
            start_walk(act, mybir.EngineType.Activation)
            with act.Fori(0, NPAIR) as j:
                for c in range(2):
                    chunk(j * 2 + c, j, c)
            chunk(NT - 1, NPAIR, 0)

            def deviation(k):
                wait(act, s_var, k + 1)
                act.activation(sd, ve, ACT.Sqrt).then_inc(s_std, 1)

            def copy_transpose(g, par):
                wait(act, s_tp, g + 1 + CR)
                wait(act, s_mm, g - 1 + CR)
                act.activation(hT[par], tp[par], ACT.Relu).then_inc(s_hT, 1)

            def first_z(n, g, par, zo):
                wait(act, s_mm, g + 1 + CR)
                act.activation(span(Z[zo], n * ZW, D), mmo[par][:, 0:D], ACT.Copy).then_inc(s_z0, 1)

            def row_phase(phase, z, ln):
                g0 = NT * phase
                if ln is not None:
                    deviation(ln)
                copy_transpose(g0, g0 % 2)

                def body(n, g, h, par):
                    if ln is not None:
                        deviation(n + ln)
                    z(n - 1, g - 1, 1 - par)
                    copy_transpose(g, par)
                tiles(act, phase, body, first=1)
                z(NT - 1, g0 + NT - 1, (g0 + NT - 1) % 2)

            row_phase(PH_PRE, lambda n, g, par: first_z(n, g, par, 0), 0)

            row_phase(PH_SAGE1, lambda n, g, par: first_z(n, g, par, 1), None)

            def whole_z(n, g, par):
                wait(act, s_mm, g + 1 + CR)
                act.activation(span(ZFULL[0], n * D, D), mmo[par][:, 0:D], ACT.Copy).then_inc(s_z0, 1)
            row_phase(PH_SAGE2, whole_z, NT)
            row_phase(PH_GCN, lambda n, g, par: first_z(n, g, par, 1), 2 * NT)

            g0, ln0 = NT * PH_INTER, 3 * NT

            def mlp(n):
                wait(act, s_tv, n + 1)
                for k in range(2):
                    a = act.activation(GT[:, 0, k * P:(k + 1) * P], tv[:, k * P:(k + 1) * P], ACT.Identity,
                                       bias=mlp_col[:, 4, k:k + 1], scale=mlp_col[:, 3, k:k + 1])
                a.then_inc(s_g0, 1)
                for l in range(3):
                    wait(act, s_q, n * 3 + (l + 1))
                    for k in range(2):
                        a = act.activation(YT[:, k * P:(k + 1) * P], mlp_ps[:, k * P:(k + 1) * P],
                                           ACT.Relu if l < 2 else ACT.Identity, bias=mlp_col[:, l, k:k + 1])
                    a.then_inc(s_y, 1)

            def edge_copy(n):
                wait(act, s_eat, n + 1)
                act.activation(eaT[:, :], mlp_ps[0:DE, 0:P], ACT.Copy).then_inc(s_eac, 1)

            def inter(n, g, par, back2=True, back1=True, here=True):
                if here:
                    edge_copy(n)
                if back2:
                    copy_transpose(g - 2, par)
                if back1:
                    mlp(n - 1)
                if here:
                    deviation(n * 3 + (ln0 - (0 if isinstance(n, int) and n == 0 else 2)))
                if back1:
                    last = isinstance(n, int) and n == NT
                    deviation(n * 3 + (ln0 - (2 if last else 1)) if not last else ln0 + 3 * NT - 2)
                    deviation(n * 3 + ln0 if not last else ln0 + 3 * NT - 1)
                if back2:
                    wait(act, s_mm, g - 1 + CR)
                    act.sem_inc(s_z0, 1)
            inter(0, g0, g0 % 2, False, False)
            inter(1, g0 + 1, (g0 + 1) % 2, False)
            with act.Fori(0, (NT - 3) // 2) as j:
                for c in range(2):
                    inter(j * 2 + (2 + c), j * 2 + (g0 + 2 + c), (g0 + c) % 2)
            inter(NT - 1, g0 + NT - 1, (g0 + NT - 1) % 2)
            inter(NT, g0 + NT, (g0 + NT) % 2, here=False)
            inter(NT + 1, g0 + NT + 1, (g0 + NT + 1) % 2, back1=False, here=False)

        @block.vector
        def _(dve):
            chain = Chain(dve, s_prep)
            dve.wait_ge(s_rows, 16 * 3 * (EB + 1))
            dve.wait_ge(s_pad, 3)
            dve.wait_ge(s_const, 7)
            whole = "p c e -> p (c e)"
            S, Dd, Wt = (rows_i[:, 0].rearrange(whole), rows_i[:, 1].rearrange(whole), rows[:, 2].rearrange(whole))
            pi = [part_i[:, a].rearrange(whole) for a in range(3)]
            pf = [part_f[:, a].rearrange(whole) for a in range(9)]
            dve.tensor_scalar(pi[0], S, 7, 4, ALU.arith_shift_right, ALU.logical_shift_left).then_inc(s_prep, 1)
            dve.tensor_scalar(pi[1], S, 127, None, ALU.bitwise_and).then_inc(s_prep, 1)
            dve.tensor_scalar(pi[2], Dd, 4, None, ALU.arith_shift_right).then_inc(s_prep, 1)
            dve.wait_ge(s_prep, 3)
            dve.tensor_copy(pf[3], pi[0]).then_inc(s_prep, 1)
            dve.tensor_scalar(pf[2], pi[1], 1.0, None, ALU.add).then_inc(s_prep, 1)
            dve.tensor_copy(pf[4], pi[2]).then_inc(s_prep, 1)
            dve.tensor_scalar(pf[1], Dd, 1.0, None, ALU.add).then_inc(s_prep, 1)
            dve.wait_ge(s_prep, 7)
            dve.tensor_scalar(pi[1], Dd, G - 1, None, ALU.bitwise_and).then_inc(s_prep, 1)
            dve.scalar_tensor_tensor(out=pf[0], in0=pf[4], scalar=float(GW), in1=pf[3], op0=ALU.mult, op1=ALU.add
                                     ).then_inc(s_prep, 1)
            dve.wait_ge(s_prep, 9)
            chain.v = 9
            chain(dve.tensor_copy(pf[3], pi[1]))
            chain(dve.scalar_tensor_tensor(out=pf[0], in0=pf[3], scalar=1.0, in1=pf[0], op0=ALU.add, op1=ALU.add))
            chain(dve.tensor_scalar(pf[6], S, float(GW), None, ALU.is_ge))
            for g in range(2, SG):
                chain(dve.scalar_tensor_tensor(out=pf[6], in0=S, scalar=float(GW * g), in1=pf[6], op0=ALU.is_ge,
                                               op1=ALU.add))
            chain(dve.tensor_tensor(pf[7], pf[4], pf[6], ALU.subtract))
            chain(dve.tensor_scalar(pf[7], pf[7], float(GW), 1.0, ALU.mult, ALU.add))
            chain(dve.tensor_tensor(pf[7], pf[7], S, ALU.add))
            chain(dve.tensor_scalar(pf[8], pf[3], float(SG), 1.0, ALU.mult, ALU.add))
            chain(dve.tensor_tensor(pf[8], pf[8], pf[6], ALU.add))
            for a, op in enumerate((ALU.max, ALU.min)):
                dve.tensor_reduce(stat[:, a, :], part_f[:, 4], AX.X, op).then_inc(s_prep, 1)
            assert chain.v + 2 == PREP_ROWS, (chain.v, PREP_ROWS)
            for a in range(6):
                dve.wait_ge(s_prep_pe, EB * (a + 1) + (2 if a > 3 else 0))
                dve.tensor_copy(col[:, a, :], ps[:, a % 4, :]).then_inc(s_prep, 1)
            dve.wait_ge(s_prep, PREP_ROWS + 6)
            w16 = ring[:, 0:NCOL]
            chain.v = PREP_ROWS + 6
            chain(dve.tensor_copy(w16, col[:, C_W0, :]))
            chain(dve.tensor_tensor(col[:, C_W1, :], col[:, C_W0, :], w16, ALU.subtract))
            chain(dve.tensor_copy(col[:, C_W0, :], w16))
            chain(dve.tensor_copy(w16, col[:, C_W1, :]))
            chain(dve.tensor_tensor(col[:, C_W2, :], col[:, C_W1, :], w16, ALU.subtract))
            chain(dve.tensor_copy(col[:, C_W1, :], w16))
            chain(dve.tensor_copy(w16, col[:, C_W2, :]))
            chain(dve.tensor_copy(col[:, C_W2, :], w16))
            hi_row, lo_row = ps[0:1, 4, 0:ET], ps[0:1, 5, 0:ET]
            big, low = scan[0:1, 0, 0:ET], scan[0:1, 1, 0:ET]
            chain(dve.tensor_copy(big, hi_row))
            chain(dve.tensor_copy(low, lo_row))
            chain(dve.tensor_tensor_scan(big, big, big, -1.0, ALU.max, ALU.max))
            chain(dve.tensor_tensor_scan(low[:, ::-1], low[:, ::-1], low[:, ::-1], 1e6, ALU.min, ALU.min))
            assert chain.v == PREP_SCAN
            dve.wait_ge(s_prep_pe, PE_TABLES + 1)
            for nb in range(2):
                first, end, both = (tab_f[:, 4 * nb + k:4 * nb + k + 1] for k in range(3))
                chain(dve.tensor_scalar(count_scratch, ps[:, 0, 0:ET], nidx[:, nb:nb + 1], None, ALU.is_lt))
                chain(dve.tensor_reduce(first, count_scratch, AX.X, ALU.add))
                chain(dve.tensor_scalar(count_scratch, ps[:, 1, 0:ET], nidx[:, nb:nb + 1], None, ALU.is_le))
                chain(dve.tensor_reduce(end, count_scratch, AX.X, ALU.add))
                chain(dve.tensor_scalar(first, first, float(ET - 1), None, ALU.min))
                chain(dve.scalar_tensor_tensor(out=end, in0=first, scalar=1.0, in1=end, op0=ALU.add, op1=ALU.max))
                chain(dve.scalar_tensor_tensor(out=both, in0=first, scalar=512.0, in1=end, op0=ALU.mult,
                                               op1=ALU.add))
            dve.wait_ge(s_prep_pe, PE_TABLES + 2)
            chain(dve.tensor_copy(tab[0:1, :], ps[0:1, 2, 0:2 * P]))
            assert chain.v == PREP_STEPS

            start_walk(dve, mybir.EngineType.DVE)
            with dve.Fori(0, NT) as c:
                def p_q_t(k, u, t, i):
                    wait(dve, s_used, k + (u + 1))
                    n = c * PER + i
                    dve.tensor_scalar(part_of(u, O_P, GW), iota1[:, :], one(off_g, n), one(col[:, C_P, :], t),
                                      ALU.add, ALU.is_equal)
                    dve.tensor_scalar(hot_t[:, u, :], iota1[:, 0:G], one(off_t, n), one(col[:, C_T, :], t),
                                      ALU.add, ALU.is_equal)
                    dve.tensor_scalar(part_of(u, O_Q, GW), iota1[:, :], one(off_g, n), one(col[:, C_Q, :], t),
                                      ALU.add, ALU.is_equal).then_inc(s_hotD, 1)
                walk(dve, mybir.EngineType.DVE, c, p_q_t)

            chain = drained(dve)
            dve.sem_inc(s_zD, CR)
            dve.sem_inc(s_aggfree, CR)

            def norm(rows_, into, eps, k, free=None):
                chain(dve.bn_stats(bn, rows_))
                chain(dve.bn_aggr(mv, bn))
                dve.tensor_scalar(ve, mv[:, 1:2], eps, None, ALU.add).then_inc(s_var, 1)
                wait(dve, s_std, k + 1)
                chain(dve.reciprocal(rs, sd))
                if free:
                    free()
                return dve.tensor_scalar(into, rows_, mv[:, 0:1], rs, ALU.subtract, ALU.mult)

            def hrow_free(g):
                wait(dve, s_tp, g - 1 + CR)

            def z_rest(n, g, par, zo, source=None):
                wait(dve, s_z0, g + 1 + CR)
                wait(dve, s_z2, g - 1 + CR)
                return dve.tensor_tensor(resid[par], mmo[par][:, 0:D], span(Z[zo], n * ZW, D), ALU.subtract)

            def agg_read(q):
                wait(dve, s_agg, q + 1 + CR)

            def agg_done():
                dve.sem_inc(s_aggfree, 1)

            def sage_post(n, g, par, zo, b):
                wait(dve, s_mm, g + 1 + CR)
                z_rest(n, g, par, zo)
                dve.tensor_tensor(node(R_, n), mmo[par][:, D:2 * D], b_early[:, b, :], ALU.add).then_inc(s_zD, 1)

            def row_phase(phase, pre, post):
                g0 = NT * phase
                pre(0, g0, g0 % 2)

                def body(n, g, h, par):
                    pre(n, g, par)
                    post(n - 1, g - 1, 1 - par)
                tiles(dve, phase, body, first=1)
                post(NT - 1, g0 + NT - 1, (g0 + NT - 1) % 2)

            dve.wait_ge(s_x, 32)
            dve.wait_ge(s_w, 16 * 16)

            def pre_first(n, g, par):
                norm(node(X, n), hrow[par], LN_EPS, n, lambda: hrow_free(g)).then_inc(s_row, 1)
            row_phase(PH_PRE, pre_first, lambda n, g, par: sage_post(n, g, par, 0, 0))

            def pre_sage1(n, g, par):
                agg_read(g - NT)
                hrow_free(g)
                a = agg[1 - par]
                chain(dve.tensor_scalar(one(rdeg, n), a[:, D:D + 1], 1.0, None, ALU.max))
                chain(dve.reciprocal(one(rdeg, n), one(rdeg, n)))
                chain(dve.scalar_tensor_tensor(out=hrow[par], in0=a[:, 0:D], scalar=one(rdeg, n),
                                               in1=node(R_, n), op0=ALU.mult, op1=ALU.add))
                dve.sem_inc(s_row, 1)
                agg_done()
            row_phase(PH_SAGE1, pre_sage1, lambda n, g, par: sage_post(n, g, par, 1, 1))

            def pre_sage2(n, g, par):
                agg_read(g - NT)
                hrow_free(g)
                chain(dve.scalar_tensor_tensor(out=urow, in0=agg[1 - par][:, 0:D], scalar=one(rdeg, n),
                                               in1=node(R_, n), op0=ALU.mult, op1=ALU.add))
                agg_done()
                chain(dve.tensor_tensor(node(X, n), node(X, n), urow, ALU.add))
                norm(node(X, n), hrow[par], LN_EPS, n + NT).then_inc(s_row, 1)

            def post_sage2(n, g, par):
                wait(dve, s_z0, g + 1 + CR)
                dve.sem_inc(s_zD, 1)
            row_phase(PH_SAGE2, pre_sage2, post_sage2)

            dve.wait_ge(s_wlate, 16 * 11)

            def pre_gcn(n, g, par):
                agg_read(g - NT)
                hrow_free(g)
                chain(dve.tensor_tensor(urow, agg[1 - par][:, 0:D], late["b_gcn"], ALU.add))
                agg_done()
                chain(dve.tensor_tensor(node(X, n), node(X, n), urow, ALU.add))
                chain(norm(node(X, n), urow, LN_EPS, n + 2 * NT))
                dve.tensor_scalar(node(R_, n), urow, 0.0, None, ALU.max)
                dve.tensor_copy(hrow[par], urow).then_inc(s_row, 1)

            def post_gcn(n, g, par):
                wait(dve, s_mm, g + 1 + CR)
                z_rest(n, g, par, 1).then_inc(s_zD, 1)
            row_phase(PH_GCN, pre_gcn, post_gcn)

            g0, ln0 = NT * PH_INTER, 3 * NT

            def inner(n, g, par, ln):
                agg_read(g - NT)
                chain(dve.scalar_tensor_tensor(out=urow, in0=agg[1 - par][:, 0:D], scalar=0.0, in1=node(R_, n),
                                               op0=ALU.max, op1=ALU.add))
                agg_done()
                wait(dve, s_tv, n)
                chain(norm(urow, inner_row, LN_EPS_INTER, ln).then_inc(s_inner, 1))

            def outer(n, g, par, ln):
                wait(dve, s_tb, n + 1)
                chain(dve.tensor_tensor(urow, tb, node(R_, n), ALU.add))
                chain(norm(urow, urow, LN_EPS_INTER, ln))
                chain(dve.tensor_tensor(urow, urow, late["s_out"], ALU.mult))
                chain(dve.tensor_tensor(urow, urow, late["b_out"], ALU.add))
                chain(dve.tensor_tensor(node(X, n), node(X, n), urow, ALU.add))
                norm(node(X, n), hrow[par], LN_EPS, ln + 1, lambda: hrow_free(g)).then_inc(s_row, 1)

            def topk(n, g, par):
                wait(dve, s_mm, g + 1 + CR)
                wait(dve, s_z2, g - 1 + CR)
                chain(dve.tensor_copy(keep, mmo[par][:, 0:D]))
                from_ = keep
                for r in range(TOPK // 8):
                    chain(dve.max(out=mx8, in_=from_))
                    chain(dve.match_replace(out=urow, in_to_replace=mx8, in_values=from_, imm_value=LOWEST))
                    from_ = urow
                chain(dve.tensor_tensor(urow, urow, keep, ALU.not_equal))
                chain(dve.tensor_tensor(resid[par], keep, urow, ALU.mult))
                chain(dve.tensor_copy(span(Z[0], n * ZW, D), resid[par]))
                dve.tensor_copy(node(R_, n), mmo[par][:, D:2 * D])
                dve.tensor_tensor(resid[par], resid[par], span(Z[0], n * ZW, D), ALU.subtract).then_inc(s_zD, 1)


            def inter(n, g, par, ln, do):
                k = ln
                for what in "iok":
                    if what not in do:
                        continue
                    if what == "i":
                        inner(n, g, par, k)
                        k = k + 1
                    elif what == "o":
                        outer(n - 1, g - 1, 1 - par, k)
                        k = k + 2
                    else:
                        topk(n - 2, g - 2, par)
            inter(0, g0, g0 % 2, ln0, "i")
            inter(1, g0 + 1, (g0 + 1) % 2, ln0 + 1, "io")
            with dve.Fori(0, (NT - 3) // 2) as j:
                for c in range(2):
                    inter(j * 2 + (2 + c), j * 2 + (g0 + 2 + c), (g0 + c) % 2,
                          j * 6 + (ln0 + 4 + 3 * c), "iok")
            inter(NT - 1, g0 + NT - 1, (g0 + NT - 1) % 2, ln0 + 3 * NT - 5, "iok")
            inter(NT, g0 + NT, (g0 + NT) % 2, ln0 + 3 * NT - 2, "ok")
            inter(NT + 1, g0 + NT + 1, (g0 + NT + 1) % 2, None, "k")

            def last(n, g, h, par):
                agg_read(g - NT)
                chain(dve.scalar_tensor_tensor(out=urow, in0=agg[1 - par][:, 0:D], scalar=one(rdeg, n),
                                               in1=node(R_, n), op0=ALU.mult, op1=ALU.add))
                agg_done()
                chain(dve.tensor_tensor(node(X, n), node(X, n), urow, ALU.add).then_inc(s_done, 1))
            tiles(dve, PH_MAXK, last)

        @block.tensor
        def _(pe):
            pe.sem_inc(s_used, RING)
            pe.sem_inc(s_tp, CR)
            pe.sem_inc(s_mm, CR)
            pe.sem_inc(s_agg, CR)
            pe.wait_ge(s_const, 7)
            pe.wait_ge(s_prep, PREP_ROWS)

            def transpose_rows_of(a, from_):
                for c in range(EB):
                    pe.transpose(ps[:, a % 4, c * P:(c + 1) * P], from_[:, c, :], ident[:, :]).then_inc(s_prep_pe, 1)
            for a, from_ in enumerate((part_f[:, 0], part_f[:, 1], part_f[:, 2], rows[:, 2])):
                transpose_rows_of(a, from_)
            for a in range(2):
                for c in range(EB):
                    m = pe.matmul(ps[0:1, 4 + a, c * P:(c + 1) * P], stat[:, a, c:c + 1], ident[:, :],
                                  start=True, stop=True, skip_group_check=True)
                m.then_inc(s_prep_pe, 1)
            for a, from_ in ((4, part_f[:, 8]), (5, part_f[:, 7])):
                pe.wait_ge(s_prep, PREP_ROWS + a - 3)
                transpose_rows_of(a, from_)
            pe.wait_ge(s_prep, PREP_SCAN)
            for k in range(2):
                m = pe.matmul(ps[:, k, 0:ET], ones_row[0:1, :], scan[0:1, k, 0:ET], start=True, stop=True)
            m.then_inc(s_prep_pe, 1)
            pe.wait_ge(s_prep, PREP_STEPS - 1)
            for k, t in enumerate((2, 6)):
                m = pe.matmul(ps[0:1, 2, k * P:(k + 1) * P], tab_f[:, t:t + 1], ident[:, :], start=True, stop=True,
                              skip_group_check=True)
            m.then_inc(s_prep_pe, 1)
            pe.wait_ge(s_prep, PREP_STEPS)

            def clear(bank):
                return pe.matmul(bank[:, 500:501], zeros[:, :], zeros[:, 0:1], start=True, stop=True,
                                 skip_group_check=True)

            pe.wait_ge(s_raw, 16 * (-(-(ET - 1) // -(-(ET - 1) // RLOADS)) + 1))
            start_walk(pe, mybir.EngineType.PE)
            with pe.Fori(0, NT) as c:
                def begin(i):
                    wait(pe, s_taken, c * PER + (i - 1 + CR))
                    clear(cnt_ps[i % 2])
                    clear(wgt_ps[i % 2])

                def add(k, u, t, i):
                    def product(out_, left, right):
                        return pe.matmul(out_, left, right, start=False, stop=True, skip_group_check=True)
                    wait(pe, s_hotD, k + (u + 1))
                    wait(pe, s_hotP, k + (u + 1))
                    product(cnt_ps[i % 2][:, 0:GW], part_of(u, O_R, P), part_of(u, O_P, GW))
                    product(cnt_ps[i % 2][0:G, GW:GW + DE], hot_t[:, u, :], node(raw, t))
                    wait(pe, s_hotA, k + (u + 1))
                    for a in range(3):
                        m = product(wgt_ps[i % 2][:, 0:GW], part_of(u, O_SW + a * P, P), part_of(u, O_Q, GW))
                    m.then_inc(s_used, 1)

                def end(i):
                    pe.matmul(cnt_ps[i % 2][:, 501:502], zeros[:, :], zeros[:, 0:1], start=False, stop=True,
                              skip_group_check=True).then_inc(s_built, 1)
                walk(pe, mybir.EngineType.PE, c, add, before=begin, after=end)
            pe.wait_ge(s_taken, NG + CR)

            def transpose_rows(g, par):
                wait(pe, s_row, g + 1)
                wait(pe, s_hT, g - 1 + CR)
                for k in range(2):
                    m = pe.transpose(tp[par][:, k * P:(k + 1) * P], hrow[par][:, k * P:(k + 1) * P], ident[:, :])
                m.then_inc(s_tp, 1)

            def multiply(g, par, W):
                wait(pe, s_hT, g + 1 + CR)
                wait(pe, s_z0, g - 1 + CR)
                wait(pe, s_zD, g - 1 + CR)
                width = W.shape[2]
                for k in range(2):
                    m = pe.matmul(mmo[par][:, 0:width], hT[par][:, k * P:(k + 1) * P], W[:, k, :],
                                  start=(k == 0), stop=(k == 1))
                m.then_inc(s_mm, 1)

            pe.wait_ge(s_w, 16 * 16)

            def pre(n, g, h, par):
                transpose_rows(g, par)
                multiply(g, par, W_early[:, 0])
            tiles(pe, PH_PRE, pre)

            def aggregate(i, n, q, h, par, b0, b1):
                if b0 == 0:
                    wait(pe, s_blk[par], h * 16 + 16)
                    wait(pe, s_aggfree, q - 1 + CR)
                for b in range(b0, b1):
                    if i == 2:
                        m = pe.matmul(agg[par][:, 0:D], BLK32[par][:, b * P:(b + 1) * P],
                                      ZFULL[0][:, b * D:(b + 1) * D], start=(b == 0), stop=(b == NT - 1),
                                      skip_group_check=True)
                        continue
                    for part in (2, 1, 0):
                        wide = D + 1 if i == 0 and part == 2 else D
                        m = pe.matmul(agg[par][:, 0:wide], BLK16[par][:, b * P:(b + 1) * P],
                                      Z[zin(i)][:, b * ZW + part * D:b * ZW + part * D + wide],
                                      start=(b == 0 and part == 2), stop=(b == NT - 1 and part == 0),
                                      skip_group_check=True)
                if b1 == NT:
                    m.then_inc(s_agg, 1)

            def z_ready(phase):
                for s in (s_z0, s_zD, s_z2):
                    pe.wait_ge(s, NT * (phase + 1) + CR)

            def row_layer(i, W):
                phase = i + 1
                z_ready(i)
                q0, g0 = NT * i, NT * phase
                aggregate(i, 0, q0, q0 // 2, q0 % 2, 0, NT)

                def body(n, q, h, par):
                    aggregate(i, n, q, h, par, 0, 12)
                    transpose_rows(q + (NT - 1), par)
                    aggregate(i, n, q, h, par, 12, 18)
                    multiply(q + (NT - 1), par, W)
                    aggregate(i, n, q, h, par, 18, NT)
                tiles(pe, i, body, first=1)
                g = g0 + NT - 1
                transpose_rows(g, g % 2)
                multiply(g, g % 2, W)

            row_layer(0, W_early[:, 1])
            pe.wait_ge(s_wlate, 16 * 11)
            row_layer(1, wk(late["W_gcn"], D))
            row_layer(2, wk(late["W_msg"], D))

            i = 3
            z_ready(i)
            q0, g0 = NT * i, NT * PH_INTER
            maxk_w = wk(late["W_maxk"], 2 * D)

            def edges_in(n):
                wait(pe, s_ean, n * 16 + 16)
                pe.transpose(mlp_ps[:, 0:P], ea_now[:, :], ident[:, :]).then_inc(s_eat, 1)

            def edges_add(n, par):
                wait(pe, s_eac, n + 1)
                pe.matmul(agg[par][:, 0:D], eaT[:, :], late["W_edge"][0:DE, :], start=False, stop=False,
                          skip_group_check=True)

            def inner_transpose(n):
                wait(pe, s_inner, n + 1)
                for k in range(2):
                    m = pe.transpose(tv[:, k * P:(k + 1) * P], inner_row[:, k * P:(k + 1) * P], ident[:, :])
                m.then_inc(s_tv, 1)

            def mlp_layer(n, l):
                if l == 0:
                    wait(pe, s_g0, n + 1)
                else:
                    wait(pe, s_g, n * 3 + l)
                W = wk(late[f"mlp{l}"], D)
                for o in range(2):
                    for k in range(2):
                        m = pe.matmul(mlp_ps[:, o * P:(o + 1) * P], W[:, k, o * P:(o + 1) * P],
                                      GT[:, l % 2, k * P:(k + 1) * P], start=(k == 0), stop=(k == 1))
                m.then_inc(s_q, 1)

            def back(n):
                wait(pe, s_g, n * 3 + 3)
                for k in range(2):
                    m = pe.transpose(tb[:, k * P:(k + 1) * P], GT[:, 1, k * P:(k + 1) * P], ident[:, :])
                m.then_inc(s_tb, 1)

            def inter(n, q, h, par, here=True, back1=True, back2=True):
                cuts = [0, 3, 6, 8, 12, 16, 20, NT]
                steps = [lambda: edges_in(n) if here else None,
                         lambda: (edges_add(n, par) if here else None,
                                  transpose_rows(q + (NT - 2), 1 - par) if back2 else None),
                         lambda: inner_transpose(n - 1) if back1 else None,
                         lambda: (multiply(q + (NT - 2), 1 - par, maxk_w) if back2 else None,
                                  mlp_layer(n - 1, 0) if back1 else None),
                         lambda: mlp_layer(n - 1, 1) if back1 else None,
                         lambda: mlp_layer(n - 1, 2) if back1 else None,
                         lambda: back(n - 1) if back1 else None]
                for s, f in enumerate(steps):
                    if here:
                        aggregate(i, n, q, h, par, cuts[s], cuts[s + 1])
                    f()

            inter(0, q0, q0 // 2, q0 % 2, back1=False, back2=False)
            inter(1, q0 + 1, (q0 + 1) // 2, (q0 + 1) % 2, back2=False)
            with pe.Fori(0, (NT - 3) // 2) as j:
                for c in range(2):
                    inter(j * 2 + (2 + c), j * 2 + (q0 + 2 + c), j + (q0 + 2 + c) // 2, (q0 + c) % 2)
            q = q0 + NT - 1
            inter(NT - 1, q, q // 2, q % 2)
            inter(NT, q + 1, None, (q + 1) % 2, here=False)
            inter(NT + 1, q + 2, None, (q + 2) % 2, here=False, back1=False)

            z_ready(4)
            tiles(pe, 4, lambda n, q, h, par: aggregate(4, n, q, h, par, 0, NT))




_WEIGHTS = ["L0_gnn_W_l1", "L0_gnn_b1", "L0_gnn_W_r1", "L0_gnn_W_l2", "L0_gnn_b2", "L0_gnn_W_r2", "L1_gnn_W",
            "L1_gnn_b", "L2_gnn_W_message", "L2_gnn_mlp_W0", "L2_gnn_mlp_b0", "L2_gnn_mlp_W1", "L2_gnn_mlp_b1",
            "L2_gnn_mlp_W2", "L2_gnn_mlp_b2", "L2_gnn_ln_aggr_scale", "L2_gnn_ln_aggr_bias", "L2_gnn_ln_out_scale",
            "L2_gnn_ln_out_bias", "L3_gnn_W_self", "L3_gnn_W_neigh"]
_INPUTS = ["x", "src", "dst", "edge_attr_64", "edge_weight"] + _WEIGHTS


def kernel(**inputs):
    import concourse.bacc as bacc
    from concourse.bass_utils import run_bass_kernel_spmd as run

    nc = bacc.Bacc("TRN2", target_bir_lowering=False, num_devices=1)
    arrays, aps = {}, {}
    for name in _INPUTS:
        arrays["in_" + name] = np.ascontiguousarray(inputs[name])
        a = arrays["in_" + name]
        aps[name] = nc.dram_tensor("in_" + name, a.shape, mybir.dt.from_np(a.dtype), kind="ExternalInput").ap()
    out = nc.dram_tensor("out_0", (N, D), F32, kind="ExternalOutput").ap()
    build(nc, aps["x"], aps["src"], aps["dst"], aps["edge_attr_64"], aps["edge_weight"],
          {k: aps[k] for k in _WEIGHTS}, out)
    return run(nc, [arrays], core_ids=[0]).results[0]["out_0"]
```

```python
from contextlib import ExitStack

import numpy as np
import concourse.bass as bass
from concourse import mybir
from concourse.alu_op_type import AluOpType as ALU

F32, F16, BF16, I32 = mybir.dt.float32, mybir.dt.float16, mybir.dt.bfloat16, mybir.dt.int32
ACT = mybir.ActivationFunctionType
AX = mybir.AxisListType

P = 128
N, D, E, DE = 3125, 256, 50000, 64
NT = -(-N // P)
NR = N - (NT - 1) * P
ET = -(-E // P)
ER = E - (ET - 1) * P
EB = -(-ET // P)
G = 16
PER = P // G
NG = NT * PER
GW = NT * G
SG = P // G
TOPK = 32
PAD_DST = 4095
ZW = 2 * D + 2
RING = 3
O_P, O_Q, O_R, O_S, O_SW = 0, GW, 2 * GW, 2 * GW + P, 2 * GW + 2 * P
SETW = 2 * GW + 5 * P
RT = ET + RING - 1
RLOADS = 6
NPAIR = NT // 2
ON_DVE = 1
CR = 2
PH_START, PH_SAGE1, PH_SAGE2, PH_GCN, PH_INTER, PH_MAXK = range(6)
LN_EPS, LN_EPS_INTER = 1e-5, 1e-6
SCALE_CONV = 8 + 1 + 5 + 5
SCALES = SCALE_CONV + 2 * 10
H_SCALE = 2048.0
SB = 5
LOWEST = -3.4e38
PREP_ROWS = 12 + (SG - 2) + 5 + 2
PREP_SCAN = PREP_ROWS + 6 + 8 + 4
PREP_STEPS = PREP_SCAN + 14 + 1
PE_EXTREMES = 4 * EB + 2
PE_TABLES = PE_EXTREMES + 2 * EB


def build(nc, x, src, dst, edge_attr, edge_weight, w, out):
    ctx = ExitStack()
    with ctx:
        def sb(name, shape, dt):
            return ctx.enter_context(nc.sbuf_tensor(name, shape, dt))

        def sem(name):
            return ctx.enter_context(nc.semaphore(name))

        cnt_dram = nc.dram_tensor("cnt_blocks", (NT, P, NT * P), F16, kind="Internal").ap()
        wgt_dram = nc.dram_tensor("wgt_blocks", (NT * P, NT * P), F32, kind="Internal").ap()
        ea_dram = nc.dram_tensor("edge_sums", (NT * P, DE), F32, kind="Internal").ap()

        XW, ZF = NT * D, NT * ZW // 2
        BLKF = NT * P
        ROW0 = 3 * EB * P
        o_raw = 2 * ROW0 + 9 * EB * P
        o_sw = o_raw + RT * DE
        arena = sb("arena", [P, max(2 * XW + 2 * ZF + 2 * BLKF, o_sw + 2 * BLKF)], F32)

        def region(at, words):
            return arena[:, at:at + words]

        o_r, o_z0, o_z1, o_blk = XW, 2 * XW, 2 * XW + ZF, 2 * XW + 2 * ZF
        X = region(0, XW).rearrange("p (n d) -> p n d", d=D)
        R_ = region(o_r, XW).rearrange("p (n d) -> p n d", d=D)
        ZH = [region(o, ZF).bitcast(F16) for o in (o_z0, o_z1)]
        ZFULL = [region(o, XW) for o in (o_z0, o_z1)]
        BLK32 = [region(o_blk + b * BLKF, BLKF) for b in range(2)]
        BLK16 = [region(o_blk + b * BLKF, BLKF // 2).bitcast(F16) for b in range(2)]
        rows = region(0, 3 * EB * P).rearrange("p (a c e) -> p a c e", a=3, c=EB)
        rows_i = rows.bitcast(I32)
        part_i = region(ROW0, 3 * EB * P).bitcast(I32).rearrange("p (a c e) -> p a c e", a=3, c=EB)
        part_f = region(2 * ROW0, 9 * EB * P).rearrange("p (a c e) -> p a c e", a=9, c=EB)
        raw = region(o_raw, RT * DE).rearrange("p (t f) -> p t f", f=DE)
        stage_w = [region(o_sw + b * BLKF, BLKF).rearrange("p (t s) -> p t s", s=GW) for b in range(2)]
        stage_e = [arena[0:G, XW + b * PER * DE:XW + (b + 1) * PER * DE].rearrange("p (t f) -> p t f", f=DE)
                   for b in range(2)]
        assert XW + 2 * PER * DE <= o_raw

        NCOL = EB * P
        front = sb("front", [P, 8 * NCOL + RING * SETW // 2], F32)
        col = front[:, 0:8 * NCOL].rearrange("p (a t) -> p a t", a=8)
        C_P, C_T, C_R, C_W0, C_S, C_Q, C_W1, C_W2 = range(8)
        ring = front[:, 8 * NCOL:].bitcast(BF16)
        late = {}
        at = 0
        for name, width in (("W_gcn", 2 * D), ("W_msg", 2 * D), ("W_maxk", 4 * D), ("mlp0", 2 * D), ("mlp1", 2 * D),
                            ("mlp2", 2 * D), ("W_edge", D), ("b_gcn", D), ("s_out", D), ("b_out", D)):
            late[name] = front[:, at:at + width]
            at += width

        def wk(ap, n):
            return ap.rearrange("p (k n) -> p k n", n=n)

        W_early = sb("W_early", [P, 2, 2, 2 * D], F32)
        b_early = sb("b_early", [P, 2, D], F32)
        mlp_col = sb("mlp_col", [P, 5, 2], F32)
        ident = sb("ident", [P, P], F32)
        iota1 = sb("iota1", [P, GW], F16)
        off_g = sb("off_g", [P, NG], F32)
        off_t = sb("off_t", [P, NG], F32)
        s_col = sb("s_t_col", [P, 2, RING], F32)
        hot_t = sb("hot_t", [P, RING, G], F32)
        nidx = sb("nidx", [P, 2], F32)
        zeros = sb("zeros", [P, P], BF16)
        ones_row = sb("ones_row", [1, P], F32)
        work = sb("work", [P, 13, D], F32)
        stage_c = [work[:, :, :].rearrange("p a d -> p (a d)")[
            :, b * BLKF // 2:(b + 1) * BLKF // 2].bitcast(F16).rearrange("p (b d) -> p b d", d=P) for b in range(2)]
        hrow = [work[:, b, :] for b in range(2)]
        hT = [work[:, 2 + b, :] for b in range(2)]
        top_row = work[:, 4, :]
        GT = work[:, 6:8, :]
        YT = work[:, 8, :]
        urow = work[:, 9, :]
        inner_row, keep, cand = (work[:, k, :] for k in (10, 11, 12))
        count_scratch = work[:, 8:10, :].rearrange("p a d -> p (a d)")[:, 0:ET]
        bn_all = work[:, 0, 0:6 * NT].rearrange("p (n s) -> p n s", s=6)
        mv_all = work[:, 1, 0:2 * NT].rearrange("p (n s) -> p n s", s=2)
        ve_all, sd_all, rs_all = (work[:, k, 0:NT] for k in (2, 3, 4))
        mean_own = work[:, 6:8, :].rearrange("p a d -> p (a d)")
        mean_ownT = work[:, 10:12, :].rearrange("p a d -> p (a d)")
        small = sb("small", [P, 32], F32)
        bn, mv, ve, sd, rs, mx8 = (small[:, 0:6], small[:, 6:8], small[:, 8:9], small[:, 9:10], small[:, 10:11],
                                   small[:, 16:24])
        scale_f = sb("scale", [P, 3, 12], F32)
        scale_i = scale_f[:, :, :].bitcast(I32)
        (conv_scale, conv_back), (top_scale, top_back), (msg_scale, msg_back) = (
            (scale_f[:, k, 8:9], scale_f[:, k, 9:10]) for k in range(3))
        rdeg_conv = sb("rdeg_conv", [P, NT], F32)
        rdeg = sb("rdeg", [P, NT], F32)
        stat = sb("stat", [P, 2, EB], F32)
        scan = work[0:1, 4:8, :].rearrange("o (a b) d -> o a (b d)", a=2)
        tab_f = sb("tab_f", [P, 8], F32)
        tab = sb("tab", [1, 2 * P], I32)
        ea_now = sb("ea_now", [P, P], F32)
        eaT = sb("eaT", [DE, P], F32)

        ps = ctx.enter_context(nc.psum_tensor("ps", [P, 8, 512], F32))
        agg = [ps[:, b, :] for b in range(2)]
        tp = [ps[:, 2 + b, 0:D] for b in range(2)]
        mmo = [ps[:, 4 + b, :] for b in range(2)]
        mlp_ps = ps[:, 6, 0:D]
        conv_t, conv_ps = ps[:, 6, :], ps[:, 7, 0:D]
        tv = ps[:, 7, 0:D]
        tb = [ps[:, 2 + b, D:2 * D] for b in range(2)]
        cnt_ps = [ps[:, b, :] for b in range(2)]
        wgt_ps = [ps[:, 2 + b, :] for b in range(2)]

        s_const = sem("constants_ready")
        s_rows = sem("edge_rows_loaded")
        s_pad = sem("padding_set")
        s_prep = sem("dve_prep_step")
        s_prep_pe = sem("pe_prep_step")
        s_raw = sem("edge_features_loaded")
        s_hotD = sem("p_q_r_ready")
        s_hotS = sem("s_ready")
        s_hotS_dve = sem("s_of_dve_ready")
        s_hotT = sem("destination_onehot_ready")
        s_hotA = sem("weighted_s_ready")
        s_made = sem("sets_begun_by_pool")
        s_used = sem("onehots_used")
        s_built = sem("tile_built")
        s_taken = sem("built_counts_taken")
        s_takenW = sem("built_weights_taken")
        s_store_c = [sem(f"count_block_stored{b}") for b in range(2)]
        s_store_w = [sem(f"weight_block_stored{b}") for b in range(2)]
        s_store_e = [sem(f"edge_sums_stored{b}") for b in range(2)]
        s_w = sem("early_weights_loaded")
        s_wlate = sem("late_weights_loaded")
        s_x = [sem(f"x_loaded{j}") for j in range(NT // SB)]
        s_xpad = sem("x_padding_set")
        s_ones = sem("degree_ones_set")
        s_blk = [sem(f"block_loaded{b}") for b in range(2)]
        s_agg = sem("aggregated")
        s_aggfree = sem("aggregate_read")
        s_var = sem("variance_ready")
        s_std = sem("deviation_ready")
        s_row = sem("rows_normalised")
        s_tp = sem("rows_transposed")
        s_hT = sem("transpose_copied")
        s_mm = sem("rows_multiplied")
        s_z0 = sem("first_part_ready")
        s_zD = sem("rows_of_dve_ready")
        s_z2 = sem("first_norm_second_part_ready")
        s_mo = sem("mean_and_own_ready")
        s_moT = sem("mean_and_own_transposed")
        s_moC = sem("mean_and_own_copied")
        s_conv = sem("convolution_multiplied")
        s_scale = sem("scale_step")
        s_scale_pe = sem("scale_pe_step")
        s_inner = sem("inner_norm_ready")
        s_tv = sem("inner_rows_transposed")
        s_g0 = sem("inner_rows_copied")
        s_q = sem("mlp_layer_multiplied")
        s_y = sem("mlp_layer_activated")
        s_g = sem("mlp_layer_added")
        s_tb = sem("mlp_rows_back")
        s_ean = sem("edge_sums_at_hand")
        s_eat = sem("edge_sums_transposed")
        s_eac = sem("edge_transpose_copied")
        s_done = sem("rows_final")
        s_out = sem("output_stored")

        block = ctx.enter_context(nc.Block())

        def wait(e, s, v):
            if not isinstance(v, int):
                e.wait_ge(s, e.snap(v))
            elif v > 0:
                e.wait_ge(s, v)

        def staggered(e, phase, body):
            g0 = NT * phase
            for n in range(2):
                body(n, g0 + n, (g0 + n) % 2, n // 2, True, n > 0, False)
            with e.Fori(0, (NT - 3) // 2) as j:
                for c in range(2):
                    body(j * 2 + (2 + c), j * 2 + (g0 + 2 + c), (g0 + c) % 2, j + 1, True, True, True)
            for n in range(NT - 1, NT + 2):
                body(n, g0 + n, (g0 + n) % 2, n // 2, n < NT, n <= NT, True)

        class Chain:

            def __init__(self, e, s):
                self.e, self.s, self.v = e, s, 0

            def __call__(self, ins):
                ins.then_inc(self.s, 1)
                self.v += 1
                self.e.wait_ge(self.s, self.v)

        def drained(e):
            def step(ins):
                e.drain()
            return step

        def tiles(e, phase, body, first=0):
            k0 = NT * phase + first
            with e.Fori(0, (NT - first) // 2) as j:
                for c in range(2):
                    body(j * 2 + (first + c), j * 2 + (k0 + c), j + (k0 + c) // 2, (k0 + c) % 2)
            if (NT - first) % 2:
                g = NT * phase + NT - 1
                body(NT - 1, g, g // 2, g % 2)

        def one(ap, n):
            return ap[:, n:n + 1] if isinstance(n, int) else ap[:, bass.ds(n, 1)]

        def span(ap, start, width):
            return ap[:, start:start + width] if isinstance(start, int) else ap[:, bass.ds(start, width)]

        def node(ap, n):
            return ap[:, n, :] if isinstance(n, int) else ap[:, bass.ds(n, 1), :].rearrange("p a d -> p (a d)")

        def bounded(v, low, high):
            return nc.s_assert_within(v, low, high, skip_runtime_bounds_check_because="the table is clamped to it")

        def zin(i):
            return i % 2

        def part_of(u, at, width):
            return ring[:, u * SETW + at:u * SETW + at + width]

        step_of = {}

        def walk(e, kind, c, per_edge_tile, after=None, before=None):
            _, packed = nc.values_load_multi_w_load_instructions(
                tab[0:1, c * PER:(c + 1) * PER] if isinstance(c, int) else tab[0:1, bass.ds(c * PER, PER)],
                engines=[kind], min_val=1, max_val=(ET - 1) * 512 + ET,
                skip_runtime_bounds_check_because="the table is clamped to it")
            for i in range(PER):
                lo = bounded(e.snap(packed[i] >> 9), 0, ET - 1)
                hi = bounded(e.snap(packed[i] & 511), 1, ET)
                if before:
                    before(i)
                with e.Fori(lo, hi, RING) as t:
                    k = e.snap(step_of[kind], min_val=0, max_val=1 << 20)
                    for u in range(RING):
                        per_edge_tile(k, u, t + u, i)
                    e.reg_add(step_of[kind], step_of[kind], RING)
                if after:
                    after(i)

        def one_tile_late(take, c, par):
            def after(t):
                if t:
                    take(c, par, t - 1)
                elif not isinstance(c, int):
                    take(c - 1, 1 - par, PER - 1)
            return after

        def start_walk(e, kind):
            step_of[kind] = e.alloc_register("sets")
            e.reg_mov(step_of[kind], 0)

        @block.sync
        def _(sp):
            sp.wait_ge(s_pad, 3)
            full = (E // P) // P * P
            for a, t in enumerate((src, dst, edge_weight)):
                into = rows_i if a < 2 else rows
                for c in range(EB - 1):
                    sp.dma_start(into[:, a, c, :], t[c * P * P:(c + 1) * P * P].rearrange("(p e) -> p e", e=P)
                                 ).then_inc(s_rows, 16)
                sp.dma_start(into[0:ET - 1 - full, a, EB - 1, :],
                             t[full * P:(ET - 1) * P].rearrange("(p e) -> p e", e=P)).then_inc(s_rows, 16)
                sp.dma_start(into[ET - 1 - full:ET - full, a, EB - 1, 0:ER],
                             t[(ET - 1) * P:E].rearrange("(p e) -> p e", p=1)).then_inc(s_rows, 16)
            for i, (l, r, b) in enumerate((("W_l1", "W_r1", "b1"), ("W_l2", "W_r2", "b2"))):
                for h, name in enumerate((l, r)):
                    sp.dma_start(W_early[:, i, :, h * D:(h + 1) * D],
                                 w["L0_gnn_" + name].rearrange("(k p) n -> p k n", p=P)).then_inc(s_w, 16)
                sp.dma_start(b_early[:, i, :], w["L0_gnn_" + b].rearrange("(o n) -> o n", o=1).broadcast_to([P, D])
                             ).then_inc(s_w, 16)
            for i, name in enumerate(("mlp_b0", "mlp_b1", "mlp_b2", "ln_aggr_scale", "ln_aggr_bias")):
                for k in range(2):
                    sp.dma_start(mlp_col[:, i, k:k + 1],
                                 w["L2_gnn_" + name][k * P:(k + 1) * P].rearrange("(p o) -> p o", o=1)
                                 ).then_inc(s_w, 16)

            sp.wait_ge(s_xpad, 1)
            for j, at in enumerate(range(0, NT, SB)):
                n = min(SB, NT - 1 - at)
                sp.dma_start(X[:, at:at + n, :], x[at * P:(at + n) * P, :].rearrange("(n p) d -> p n d", p=P)
                             ).then_inc(s_x[j], 16)
            sp.dma_start(X[0:NR, NT - 1, :], x[(NT - 1) * P:N, :]).then_inc(s_x[NT // SB - 1], 16)

            def store(c, par):
                wait(sp, s_taken, c * PER + (PER + CR))
                wait(sp, s_takenW, c * PER + (PER + CR))
                dc = cnt_dram[c] if isinstance(c, int) else cnt_dram[bass.ds(c, 1)].rearrange("o p f -> (o p) f")
                rows_of = wgt_dram[bass.ds(c * P, P), :]
                sp.dma_start(dc, stage_c[par].rearrange("p b d -> p (b d)")).then_inc(s_store_c[par], 16)
                sp.dma_start(rows_of.rearrange("(t d) (g s) -> (d g) t s", d=G, g=SG), stage_w[par]
                             ).then_inc(s_store_w[par], 16)
                sp.dma_start(ea_dram[bass.ds(c * P, P), :].rearrange("(t d) f -> d t f", d=G), stage_e[par]
                             ).then_inc(s_store_e[par], 16)

            with sp.Fori(0, NPAIR) as j:
                for c in range(2):
                    store(j * 2 + c, c)
            store(NT - 1, 0)

            sp.wait_ge(s_built, NG)
            for name, of in (("W_gcn", "L1_gnn_W"), ("mlp0", "L2_gnn_mlp_W0"), ("mlp1", "L2_gnn_mlp_W1"),
                             ("mlp2", "L2_gnn_mlp_W2")):
                sp.dma_start(wk(late[name], D), w[of].rearrange("(k p) n -> p k n", p=P)).then_inc(s_wlate, 16)
            sp.dma_start(wk(late["W_msg"], D), w["L2_gnn_W_message"][0:D, :].rearrange("(k p) n -> p k n", p=P)
                         ).then_inc(s_wlate, 16)
            sp.dma_start(late["W_edge"][0:DE, :], w["L2_gnn_W_message"][D:D + DE, :]).then_inc(s_wlate, 16)
            for h, of in enumerate(("L3_gnn_W_neigh", "L3_gnn_W_self")):
                sp.dma_start(wk(late["W_maxk"], 2 * D)[:, :, h * D:(h + 1) * D],
                             w[of].rearrange("(k p) n -> p k n", p=P)).then_inc(s_wlate, 16)
            for name, of in (("b_gcn", "L1_gnn_b"), ("s_out", "L2_gnn_ln_out_scale"), ("b_out", "L2_gnn_ln_out_bias")):
                sp.dma_start(late[name], w[of].rearrange("(o n) -> o n", o=1).broadcast_to([P, D])
                             ).then_inc(s_wlate, 16)

            for par in range(2):
                uses = (NT + 1 - par) // 2
                sp.wait_ge(s_store_c[par], 16 * uses)
                sp.wait_ge(s_store_w[par], 16 * uses)
                sp.wait_ge(s_store_e[par], 16 * uses)
            for i in range(5):
                def load(n, q, h, par, i=i):
                    wait(sp, s_agg, q + 1)
                    if i == 2:
                        cols = wgt_dram[:, bass.ds(n * P, P)].rearrange("(b p) s -> p b s", p=P)
                        sp.dma_start(BLK32[par].rearrange("p (b s) -> p b s", s=P), cols).then_inc(s_blk[par], 16)
                    else:
                        f = cnt_dram[n] if isinstance(n, int) else \
                            cnt_dram[bass.ds(n, 1)].rearrange("o p f -> (o p) f")
                        sp.dma_start(BLK16[par], f).then_inc(s_blk[par], 16)
                    if i == 3:
                        wait(sp, s_eat, n)
                        sp.dma_start(ea_now[:, 0:DE], ea_dram[bass.ds(n * P, P), :]).then_inc(s_ean, 16)
                tiles(sp, i, load)

            def store_out(n, g, h, par):
                wait(sp, s_done, n + 1)
                sp.dma_start(out[bass.ds(n * P, P), :], node(X, n)).then_inc(s_out, 16)

            with sp.Fori(0, NT - 1) as n:
                store_out(n, 0, 0, 0)
            sp.wait_ge(s_done, NT)
            sp.dma_start(out[(NT - 1) * P:N, :], X[0:NR, NT - 1, :]).then_inc(s_out, 16)
            sp.wait_ge(s_out, 16 * NT)

        @block.gpsimd
        def _(pool):
            chain = drained(pool)
            pool.memset(rows_i[:, 0, EB - 1, :], 0).then_inc(s_pad, 1)
            pool.memset(rows_i[:, 1, EB - 1, :], PAD_DST).then_inc(s_pad, 1)
            pool.memset(rows[:, 2, EB - 1, :], 0.0).then_inc(s_pad, 1)
            pool.memset(raw[:, ET - 1:RT, :], 0.0).then_inc(s_pad, 1)
            chain(pool.memset(ident[:, :], 0.0))
            pool.affine_select(out=ident[:, :], in_=ident[:, :], compare_op=ALU.not_equal, fill=1.0, base=0,
                               pattern=[[-1, P]], channel_multiplier=1).then_inc(s_const, 1)
            pool.iota(iota1[:, :], pattern=[[1, GW]], base=1, channel_multiplier=0,
                      allow_small_or_imprecise_dtypes=True).then_inc(s_const, 1)
            pool.iota(off_g[:, :], pattern=[[GW, NG]], base=0, channel_multiplier=0,
                      allow_small_or_imprecise_dtypes=True).then_inc(s_const, 1)
            pool.iota(off_t[:, :], pattern=[[G, NG]], base=0, channel_multiplier=0,
                      allow_small_or_imprecise_dtypes=True).then_inc(s_const, 1)
            pool.iota(nidx[:, :], pattern=[[P, 2]], base=0, channel_multiplier=1,
                      allow_small_or_imprecise_dtypes=True).then_inc(s_const, 1)
            pool.memset(zeros[:, :], 0.0).then_inc(s_const, 1)
            pool.memset(ea_now[:, :], 0.0)
            pool.memset(ones_row[:, :], 1.0).then_inc(s_const, 1)

            pool.wait_ge(s_prep, PREP_STEPS)
            pool.wait_ge(s_prep_pe, PE_TABLES + 2)
            pool.memset(X[:, NT - 1, :], 0.0).then_inc(s_xpad, 1)
            start_walk(pool, mybir.EngineType.Pool)
            with pool.Fori(0, NT) as c:
                def hot_s_t(k, u, t, i):
                    if u == 0:
                        pool.drain()
                        pool.tensor_copy(s_col[:, 0, :], col[:, C_S, bass.ds(t, RING)])
                        chain(pool.tensor_tensor(s_col[:, 1, :], col[:, C_T, bass.ds(t, RING)],
                                                 one(off_t, c * PER + i).broadcast_to([P, RING]), ALU.subtract))
                    wait(pool, s_used, k + (u + 1))
                    pool.sem_inc(s_made, 1)
                    if u != ON_DVE:
                        pool.tensor_scalar(part_of(u, O_S, P), iota1[:, 0:P], s_col[:, 0, u:u + 1], None,
                                           ALU.is_equal).then_inc(s_hotS, 2 if u == ON_DVE + 1 else 1)
                    pool.tensor_scalar(hot_t[:, u, :], iota1[:, 0:G], s_col[:, 1, u:u + 1], None, ALU.is_equal
                                       ).then_inc(s_hotT, 1)
                walk(pool, mybir.EngineType.Pool, c, hot_s_t)

            pool.wait_ge(s_built, NG)
            pool.memset(ZH[0].rearrange("p (n k) -> p n k", k=ZW)[:, :, 2 * D:2 * D + 2], 1.0).then_inc(s_ones, 1)

            def second(n):
                wait(pool, s_z0, n + 1 + CR)
                pool.sem_inc(s_made, 1)
                pool.tensor_tensor(span(ZH[0], n * ZW + D, D), node(R_, n), span(ZH[0], n * ZW, D), ALU.subtract
                                   ).then_inc(s_z2, 1)
            with pool.Fori(0, NT // SB) as j:
                for c in range(SB):
                    second(j * SB + c)

            def mlp_sums(n):
                for l in range(3):
                    wait(pool, s_y, n * 3 + (l + 1))
                    pool.tensor_tensor(GT[:, (l + 1) % 2, :], GT[:, l % 2, :], YT, ALU.add).then_inc(s_g, 1)

            with pool.Fori(0, NT) as n:
                mlp_sums(n)

        @block.scalar
        def _(act):
            act.sem_inc(s_hT, CR + NT)
            act.sem_inc(s_z0, CR)
            act.sem_inc(s_taken, CR)

            act.wait_ge(s_rows, 16 * 3 * (EB + 1))
            per = -(-(ET - 1) // RLOADS)
            for t0 in range(0, ET - 1, per):
                t1 = min(t0 + per, ET - 1)
                act.dma_start(raw[:, t0:t1, :], edge_attr[t0 * P:t1 * P, :].rearrange("(t p) f -> p t f", p=P)
                              ).then_inc(s_raw, 16)
            act.wait_ge(s_pad, 4)
            act.dma_start(raw[0:ER, ET - 1, :], edge_attr[(ET - 1) * P:E, :]).then_inc(s_raw, 16)

            def take(c, par, t):
                wait(act, s_built, c * PER + (t + 1))
                act.activation(stage_c[par][:, :, t * G:(t + 1) * G],
                               cnt_ps[t % 2][:, 0:GW].rearrange("p (b d) -> p b d", d=G), ACT.Copy)
                act.activation(stage_e[par][:, t, :], cnt_ps[t % 2][0:G, GW:GW + DE], ACT.Copy
                               ).then_inc(s_taken, 1)

            def weigh(k, u, t, i):
                wait(act, s_hotS_dve if u == ON_DVE else s_hotS, k + (RING if u == ON_DVE else u + 1))
                for a, c in enumerate((C_W0, C_W1, C_W2)[0:3 - (u == ON_DVE)]):
                    m = act.activation(part_of(u, O_SW + a * P, P), part_of(u, O_S, P), ACT.Copy,
                                       scale=one(col[:, c, :], t))
                m.then_inc(s_hotA, 1)

            def chunk(c, half, par):
                for s in (s_store_c, s_store_e):
                    wait(act, s[par], half * 16)
                walk(act, mybir.EngineType.Activation, c, weigh, after=one_tile_late(take, c, par))
            act.wait_ge(s_prep, PREP_STEPS)
            start_walk(act, mybir.EngineType.Activation)
            chunk(0, 0, 0)
            with act.Fori(0, NPAIR) as j:
                chunk(j * 2 + 1, j, 1)
                chunk(j * 2 + 2, j + 1, 0)
            take(NT - 1, 0, PER - 1)

            def deviation(k):
                wait(act, s_var, k + 1)
                act.activation(sd, ve, ACT.Sqrt).then_inc(s_std, 1)

            def copy_transpose(g, par):
                wait(act, s_tp, g + 1 + CR)
                wait(act, s_mm, g - 1 + CR)
                act.activation(hT[par], tp[par], ACT.Relu).then_inc(s_hT, 1)

            def first_z(n, g, par, z, scale=1.0):
                wait(act, s_mm, g + 1 + CR)
                act.activation(span(z, n * ZW, D), mmo[par][:, 0:D], ACT.Copy, scale=scale).then_inc(s_z0, 1)

            def row_phase(phase, z, ln):
                g0 = NT * phase
                if ln is not None:
                    deviation(ln)
                copy_transpose(g0, g0 % 2)

                def body(n, g, h, par):
                    if ln is not None:
                        deviation(n + ln)
                    z(n - 1, g - 1, 1 - par)
                    copy_transpose(g, par)
                tiles(act, phase, body, first=1)
                z(NT - 1, g0 + NT - 1, (g0 + NT - 1) % 2)

            act.wait_ge(s_var, 1)
            act.activation(sd_all, ve_all, ACT.Sqrt).then_inc(s_std, 1)

            with act.Fori(0, NT // SB) as j:
                for c in range(SB):
                    n = j * SB + c
                    wait(act, s_zD, n + 1 + CR)
                    act.activation(span(ZH[0], n * ZW, D), node(R_, n), ACT.Copy).then_inc(s_z0, 1)

            def copy_conv(n):
                wait(act, s_moT, n + 1)
                wait(act, s_conv, n)
                act.activation(mean_ownT, conv_t, ACT.Copy, scale=1.0 / H_SCALE).then_inc(s_moC, 1)

            def sage1(n, g, par, half, at0, at1, at2):
                if at1:
                    copy_conv(n - 1)
                if at2:
                    copy_transpose(g - 2, par)
                    first_z(n - 2, g - 2, par, ZH[1], conv_scale)
            staggered(act, PH_SAGE1, sage1)

            def whole_z(n, g, par):
                wait(act, s_mm, g + 1 + CR)
                act.activation(span(ZFULL[0], n * D, D), mmo[par][:, 0:D], ACT.Copy).then_inc(s_z0, 1)
            row_phase(PH_SAGE2, whole_z, 1)
            act.wait_ge(s_scale, SCALES)
            row_phase(PH_GCN, lambda n, g, par: first_z(n, g, par, ZH[1], msg_scale), NT + 1)

            g0 = NT * PH_INTER

            ln0 = 2 * NT + 1

            def inner_rows(n):
                wait(act, s_tv, n + 1)
                for k in range(2):
                    a = act.activation(GT[:, 0, k * P:(k + 1) * P], tv[:, k * P:(k + 1) * P], ACT.Identity,
                                       bias=mlp_col[:, 4, k:k + 1], scale=mlp_col[:, 3, k:k + 1])
                a.then_inc(s_g0, 1)

            def mlp(n, l):
                wait(act, s_q, n * 3 + (l + 1))
                for k in range(2):
                    a = act.activation(YT[:, k * P:(k + 1) * P], mlp_ps[:, k * P:(k + 1) * P],
                                       ACT.Relu if l < 2 else ACT.Identity, bias=mlp_col[:, l, k:k + 1])
                a.then_inc(s_y, 1)

            def edge_copy(n):
                wait(act, s_eat, n + 1)
                act.activation(eaT[:, :], mlp_ps[0:DE, 0:P], ACT.Copy, scale=msg_scale[0:DE, :]).then_inc(s_eac, 1)

            def take_top(n, g, par):
                wait(act, s_mm, g + 1 + CR)
                wait(act, s_zD, g - 1 + CR)
                act.activation(keep, mmo[par][:, 0:D], ACT.Copy, scale=top_scale)
                act.activation(node(R_, n), mmo[par][:, D:2 * D], ACT.Copy).then_inc(s_z0, 1)

            def inter(n, g, par, back2=True, back1=True, here=True):
                if back1:
                    deviation(n * 3 + (ln0 - 5) if not (isinstance(n, int) and n == 1) else ln0)
                if here:
                    edge_copy(n)
                if back1:
                    inner_rows(n - 1)
                if back2:
                    deviation(n * 3 + (ln0 - 4) if back1 else ln0 + 3 * NT - 2)
                if back1:
                    for l in range(3):
                        mlp(n - 1, l)
                if back2:
                    deviation(n * 3 + (ln0 - 3) if back1 else ln0 + 3 * NT - 1)
                    copy_transpose(g - 2, par)
                    take_top(n - 2, g - 2, par)
            inter(0, g0, g0 % 2, False, False)
            inter(1, g0 + 1, (g0 + 1) % 2, False)
            with act.Fori(0, (NT - 3) // 2) as j:
                for c in range(2):
                    inter(j * 2 + (2 + c), j * 2 + (g0 + 2 + c), (g0 + c) % 2)
            inter(NT - 1, g0 + NT - 1, (g0 + NT - 1) % 2)
            inter(NT, g0 + NT, (g0 + NT) % 2, here=False)
            inter(NT + 1, g0 + NT + 1, (g0 + NT + 1) % 2, back1=False, here=False)

        @block.vector
        def _(dve):
            chain = Chain(dve, s_prep)
            dve.wait_ge(s_rows, 16 * 3 * (EB + 1))
            dve.wait_ge(s_pad, 3)
            dve.wait_ge(s_const, 7)
            whole = "p c e -> p (c e)"
            S, Dd = rows_i[:, 0].rearrange(whole), rows_i[:, 1].rearrange(whole)
            pi = [part_i[:, a].rearrange(whole) for a in range(3)]
            pf = [part_f[:, a].rearrange(whole) for a in range(9)]
            dve.tensor_scalar(pi[0], S, 7, 4, ALU.arith_shift_right, ALU.logical_shift_left).then_inc(s_prep, 1)
            dve.tensor_scalar(pi[1], S, 127, None, ALU.bitwise_and).then_inc(s_prep, 1)
            dve.tensor_scalar(pi[2], Dd, 4, None, ALU.arith_shift_right).then_inc(s_prep, 1)
            dve.wait_ge(s_prep, 3)
            dve.tensor_copy(pf[3], pi[0]).then_inc(s_prep, 1)
            dve.tensor_scalar(pf[2], pi[1], 1.0, None, ALU.add).then_inc(s_prep, 1)
            dve.tensor_copy(pf[4], pi[2]).then_inc(s_prep, 1)
            dve.tensor_scalar(pf[1], Dd, 1.0, None, ALU.add).then_inc(s_prep, 1)
            dve.wait_ge(s_prep, 7)
            dve.tensor_scalar(pi[1], Dd, G - 1, None, ALU.bitwise_and).then_inc(s_prep, 1)
            dve.scalar_tensor_tensor(out=pf[0], in0=pf[4], scalar=float(GW), in1=pf[3], op0=ALU.mult, op1=ALU.add
                                     ).then_inc(s_prep, 1)
            dve.wait_ge(s_prep, 9)
            chain.v = 9
            chain(dve.tensor_copy(pf[3], pi[1]))
            chain(dve.scalar_tensor_tensor(out=pf[0], in0=pf[3], scalar=1.0, in1=pf[0], op0=ALU.add, op1=ALU.add))
            chain(dve.tensor_scalar(pf[6], S, float(GW), None, ALU.is_ge))
            for g in range(2, SG):
                chain(dve.scalar_tensor_tensor(out=pf[6], in0=S, scalar=float(GW * g), in1=pf[6], op0=ALU.is_ge,
                                               op1=ALU.add))
            chain(dve.tensor_tensor(pf[7], pf[4], pf[6], ALU.subtract))
            chain(dve.tensor_scalar(pf[7], pf[7], float(GW), 1.0, ALU.mult, ALU.add))
            chain(dve.tensor_tensor(pf[7], pf[7], S, ALU.add))
            chain(dve.tensor_scalar(pf[8], pf[3], float(SG), 1.0, ALU.mult, ALU.add))
            chain(dve.tensor_tensor(pf[8], pf[8], pf[6], ALU.add))
            for a, op in enumerate((ALU.max, ALU.min)):
                dve.tensor_reduce(stat[:, a, :], part_f[:, 4], AX.X, op).then_inc(s_prep, 1)
            assert chain.v + 2 == PREP_ROWS, (chain.v, PREP_ROWS)
            for a in range(6):
                dve.wait_ge(s_prep_pe, EB * (a + 1) + (2 if a > 3 else 0))
                dve.tensor_copy(col[:, a, :], ps[:, a % 4, :]).then_inc(s_prep, 1)
            dve.wait_ge(s_prep, PREP_ROWS + 6)
            w16 = ring[:, 0:NCOL]
            chain.v = PREP_ROWS + 6
            chain(dve.tensor_copy(w16, col[:, C_W0, :]))
            chain(dve.tensor_tensor(col[:, C_W1, :], col[:, C_W0, :], w16, ALU.subtract))
            chain(dve.tensor_copy(col[:, C_W0, :], w16))
            chain(dve.tensor_copy(w16, col[:, C_W1, :]))
            chain(dve.tensor_tensor(col[:, C_W2, :], col[:, C_W1, :], w16, ALU.subtract))
            chain(dve.tensor_copy(col[:, C_W1, :], w16))
            chain(dve.tensor_copy(w16, col[:, C_W2, :]))
            chain(dve.tensor_copy(col[:, C_W2, :], w16))
            hi_row, lo_row = ps[0:1, 4, 0:ET], ps[0:1, 5, 0:ET]
            big, low = scan[0:1, 0, 0:ET], scan[0:1, 1, 0:ET]
            chain(dve.tensor_copy(big, hi_row))
            chain(dve.tensor_copy(low, lo_row))
            chain(dve.tensor_tensor_scan(big, big, big, -1.0, ALU.max, ALU.max))
            chain(dve.tensor_tensor_scan(low[:, ::-1], low[:, ::-1], low[:, ::-1], 1e6, ALU.min, ALU.min))
            assert chain.v == PREP_SCAN
            dve.wait_ge(s_prep_pe, PE_TABLES + 1)
            for nb in range(2):
                first, end, both = (tab_f[:, 4 * nb + k:4 * nb + k + 1] for k in range(3))
                chain(dve.tensor_scalar(count_scratch, ps[:, 0, 0:ET], nidx[:, nb:nb + 1], None, ALU.is_lt))
                chain(dve.tensor_reduce(first, count_scratch, AX.X, ALU.add))
                chain(dve.tensor_scalar(count_scratch, ps[:, 1, 0:ET], nidx[:, nb:nb + 1], None, ALU.is_le))
                chain(dve.tensor_reduce(end, count_scratch, AX.X, ALU.add))
                chain(dve.tensor_scalar(first, first, float(ET - 1), None, ALU.min))
                chain(dve.scalar_tensor_tensor(out=end, in0=first, scalar=1.0, in1=end, op0=ALU.add, op1=ALU.max))
                chain(dve.scalar_tensor_tensor(out=both, in0=first, scalar=512.0, in1=end, op0=ALU.mult,
                                               op1=ALU.add))
            dve.wait_ge(s_prep_pe, PE_TABLES + 2)
            chain(dve.tensor_copy(tab[0:1, :], ps[0:1, 2, 0:2 * P]))
            assert chain.v == PREP_STEPS

            dve.sem_inc(s_takenW, CR)
            start_walk(dve, mybir.EngineType.DVE)

            def take(c, par, t):
                wait(dve, s_built, c * PER + (t + 1))
                dve.tensor_copy(stage_w[par][:, t, :], wgt_ps[t % 2][:, 0:GW]).then_inc(s_takenW, 1)

            def hot_and_take(c, half, par):
                def hot(k, u, t, i):
                    wait(dve, s_used, k + (u + 1))
                    n = c * PER + i
                    if u == ON_DVE:
                        dve.tensor_scalar(part_of(u, O_S, P), iota1[:, 0:P], one(col[:, C_S, :], t), None,
                                          ALU.is_equal).then_inc(s_hotS_dve, RING)
                    dve.tensor_scalar(part_of(u, O_P, GW), iota1[:, :], one(off_g, n), one(col[:, C_P, :], t),
                                      ALU.add, ALU.is_equal)
                    dve.tensor_scalar(part_of(u, O_R, P), iota1[:, 0:P], one(col[:, C_R, :], t), None,
                                      ALU.is_equal)
                    if u == ON_DVE:
                        dve.tensor_scalar(part_of(u, O_SW + 2 * P, P), iota1[:, 0:P], one(col[:, C_S, :], t),
                                          one(col[:, C_W2, :], t), ALU.is_equal, ALU.mult)
                    dve.tensor_scalar(part_of(u, O_Q, GW), iota1[:, :], one(off_g, n), one(col[:, C_Q, :], t),
                                      ALU.add, ALU.is_equal).then_inc(s_hotD, 1)

                wait(dve, s_store_w[par], half * 16)
                walk(dve, mybir.EngineType.DVE, c, hot, after=one_tile_late(take, c, par))
            hot_and_take(0, 0, 0)
            with dve.Fori(0, NPAIR) as j:
                hot_and_take(j * 2 + 1, j, 1)
                hot_and_take(j * 2 + 2, j + 1, 0)
            take(NT - 1, 0, PER - 1)

            chain = drained(dve)
            dve.sem_inc(s_zD, CR)
            dve.sem_inc(s_aggfree, CR)

            def variance(eps):
                return dve.tensor_scalar(ve, mv[:, 1:2], eps, None, ALU.add).then_inc(s_var, 1)

            def inverse_deviation(k):
                wait(dve, s_std, k + 1)
                return dve.reciprocal(rs, sd)

            def norm(rows_, into, eps, k):
                chain(dve.bn_stats(bn, rows_))
                chain(dve.bn_aggr(mv, bn))
                variance(eps)
                chain(inverse_deviation(k))
                return dve.tensor_scalar(into, rows_, mv[:, 0:1], rs, ALU.subtract, ALU.mult)

            def hrow_free(g):
                wait(dve, s_tp, g - 1 + CR)

            def second_part(n, g, par, scale):
                wait(dve, s_z0, g + 1 + CR)
                return dve.scalar_tensor_tensor(out=span(ZH[1], n * ZW + D, D), in0=mmo[par][:, 0:D], scalar=scale,
                                                in1=span(ZH[1], n * ZW, D), op0=ALU.mult, op1=ALU.subtract)

            def agg_read(q):
                wait(dve, s_agg, q + 1 + CR)

            def agg_done():
                dve.sem_inc(s_aggfree, 1)

            def sage_post(n, g, par):
                second_part(n, g, par, conv_scale)
                dve.tensor_tensor(node(R_, n), mmo[par][:, D:2 * D], b_early[:, 1, :], ALU.add).then_inc(s_zD, 1)

            def row_phase(phase, pre, post):
                g0 = NT * phase
                pre(0, g0, g0 % 2)

                def body(n, g, h, par):
                    pre(n, g, par)
                    post(n - 1, g - 1, 1 - par)
                tiles(dve, phase, body, first=1)
                post(NT - 1, g0 + NT - 1, (g0 + NT - 1) % 2)

            dve.wait_ge(s_w, 16 * 16)

            step = Chain(dve, s_scale)

            def largest(k, at, W):
                c = scale_f[:, k]
                step(dve.tensor_reduce(c[:, 0:2], W, AX.X, ALU.max))
                step(dve.tensor_reduce(c[:, 2:4], W, AX.X, ALU.min))
                step(dve.scalar_tensor_tensor(out=c[:, 0:2], in0=c[:, 2:4], scalar=-1.0, in1=c[:, 0:2],
                                              op0=ALU.mult, op1=ALU.max))
                step(dve.tensor_reduce(c[:, at:at + 1], c[:, 0:2], AX.X, ALU.max))

            def across(k, many, pe_steps):
                dve.wait_ge(s_scale_pe, pe_steps)
                step(dve.tensor_reduce(scale_f[0:1, k, 10:10 + many],
                                       ps[0:1, 7, 0:many * P].rearrange("p (m c) -> p m c", c=P), AX.X, ALU.max))
                dve.wait_ge(s_scale_pe, pe_steps + 1)

            def powers(k, t):
                c, i = scale_f[:, k], scale_i[:, k]
                step(dve.tensor_scalar(c[:, 6:7], t, 1e-30, None, ALU.max))
                step(dve.tensor_scalar(i[:, 7:8], i[:, 6:7], 23, None, ALU.arith_shift_right))
                step(dve.tensor_scalar(i[:, 8:9], i[:, 7:8], -1.0, 260.0, ALU.mult, ALU.add))
                step(dve.tensor_scalar(i[:, 9:10], i[:, 7:8], -6.0, None, ALU.add))
                step(dve.tensor_scalar(i[:, 8:10], i[:, 8:10], 23, None, ALU.logical_shift_left))

            largest(0, 4, W_early[:, 0])
            largest(0, 5, W_early[:, 1, :, 0:D])
            bias_c = scale_f[:, 0]
            across(0, 2, 1)
            step(dve.tensor_reduce(bias_c[:, 0:1], b_early[:, 0, :], AX.X, ALU.max))
            step(dve.tensor_reduce(bias_c[:, 1:2], b_early[:, 0, :], AX.X, ALU.min))
            step(dve.scalar_tensor_tensor(out=bias_c[:, 0:1], in0=bias_c[:, 1:2], scalar=-1.0, in1=bias_c[:, 0:1],
                                          op0=ALU.mult, op1=ALU.max))
            step(dve.scalar_tensor_tensor(out=bias_c[:, 0:1], in0=ps[:, 7, 2 * P:2 * P + 1], scalar=2.0 * D,
                                          in1=bias_c[:, 0:1], op0=ALU.mult, op1=ALU.add))
            step(dve.tensor_tensor(bias_c[:, 0:1], ps[:, 7, 2 * P + 1:2 * P + 2], bias_c[:, 0:1], ALU.mult))
            powers(0, bias_c[:, 0:1])
            assert step.v == SCALE_CONV

            dve.wait_ge(s_built, NG)
            for par in range(2):
                for s in (s_store_c, s_store_e):
                    dve.wait_ge(s[par], 16 * ((NT + 1 - par) // 2))
            for j in range(NT // SB):
                dve.wait_ge(s_x[j], 16 * (1 + (j == NT // SB - 1)))
                for n in range(j * SB, (j + 1) * SB):
                    dve.bn_stats(bn_all[:, n, :], X[:, n, :])
            dve.drain()
            for n in range(NT):
                dve.bn_aggr(mv_all[:, n, :], bn_all[:, n, :])
            dve.drain()
            dve.tensor_scalar(ve_all, mv_all[:, :, 1], LN_EPS, None, ALU.add).then_inc(s_var, 1)
            dve.wait_ge(s_std, 1)
            chain(dve.reciprocal(rs_all, sd_all))
            with dve.Fori(0, NT // SB) as j:
                for c in range(SB):
                    n = j * SB + c
                    dve.tensor_scalar(node(R_, n), node(X, n), one(mv_all.rearrange("p n s -> p (n s)"), n * 2),
                                      one(rs_all, n), ALU.subtract, ALU.mult)
                dve.drain()
                for c in range(SB):
                    n = j * SB + c
                    dve.tensor_scalar(node(R_, n), node(R_, n), 0.0, H_SCALE, ALU.max, ALU.mult).then_inc(s_zD, 1)
            dve.sem_inc(s_row, NT)
            dve.drain()

            def mean_and_own(n, g, par):
                agg_read(g - NT)
                a = agg[1 - par]
                chain(dve.tensor_scalar(one(rdeg, n), a[:, D:D + 1], 1.0, None, ALU.max))
                chain(dve.reciprocal(one(rdeg, n), one(rdeg, n)))
                wait(dve, s_moT, n)
                dve.tensor_scalar(mean_own[:, 0:D], a[:, 0:D], one(rdeg, n), None, ALU.mult)
                chain(dve.tensor_copy(mean_own[:, D:2 * D], node(R_, n)).then_inc(s_mo, 1))
                agg_done()

            def convolved(n, g, par):
                wait(dve, s_conv, n + 1)
                hrow_free(g)
                dve.tensor_tensor(hrow[par], conv_ps, b_early[:, 0, :], ALU.add).then_inc(s_row, 1)

            def sage1(n, g, par, half, at0, at1, at2):
                if at0:
                    mean_and_own(n, g, par)
                if at1:
                    convolved(n - 1, g - 1, 1 - par)
                if at2:
                    sage_post(n - 2, g - 2, par)
            staggered(dve, PH_SAGE1, sage1)

            chain(dve.tensor_scalar(rdeg_conv[:, :], rdeg[:, :], conv_back, None, ALU.mult))

            def pre_sage2(n, g, par):
                agg_read(g - NT)
                hrow_free(g)
                chain(dve.scalar_tensor_tensor(out=urow, in0=agg[1 - par][:, 0:D], scalar=one(rdeg_conv, n),
                                               in1=node(R_, n), op0=ALU.mult, op1=ALU.add))
                agg_done()
                chain(dve.tensor_tensor(node(X, n), node(X, n), urow, ALU.add))
                norm(node(X, n), hrow[par], LN_EPS, n + 1).then_inc(s_row, 1)

            def post_sage2(n, g, par):
                wait(dve, s_z0, g + 1 + CR)
                dve.sem_inc(s_zD, 1)
            row_phase(PH_SAGE2, pre_sage2, post_sage2)

            dve.wait_ge(s_wlate, 16 * 11)

            W_top = wk(late["W_maxk"], 2 * D)[:, :, 0:D]
            largest(1, 4, W_top)
            across(1, 1, 3)
            powers(1, ps[:, 7, 2 * P:2 * P + 1])
            largest(2, 4, wk(late["W_msg"], D))
            across(2, 1, 5)
            powers(2, ps[:, 7, 2 * P:2 * P + 1])
            assert step.v == SCALES

            def pre_gcn(n, g, par):
                agg_read(g - NT)
                hrow_free(g)
                chain(dve.tensor_tensor(urow, agg[1 - par][:, 0:D], late["b_gcn"], ALU.add))
                agg_done()
                chain(dve.tensor_tensor(node(X, n), node(X, n), urow, ALU.add))
                chain(norm(node(X, n), urow, LN_EPS, n + NT + 1))
                dve.tensor_scalar(node(R_, n), urow, 0.0, None, ALU.max)
                dve.tensor_copy(hrow[par], urow).then_inc(s_row, 1)

            def post_gcn(n, g, par):
                second_part(n, g, par, msg_scale).then_inc(s_zD, 1)
            row_phase(PH_GCN, pre_gcn, post_gcn)

            assert TOPK == 4 * 8
            g0, ln0 = NT * PH_INTER, 2 * NT + 1

            def inner(n, g, par):
                agg_read(g - NT)
                chain(dve.tensor_scalar(urow, agg[1 - par][:, 0:D], msg_back, 0.0, ALU.mult, ALU.max))
                agg_done()
                chain(dve.tensor_tensor(urow, urow, node(R_, n), ALU.add))
                wait(dve, s_tv, n)
                chain(norm(urow, inner_row, LN_EPS_INTER, ln0 if isinstance(n, int) and n == 0 else n * 3 + (ln0 - 2)
                           ).then_inc(s_inner, 1))

            def outer_and_top(n, g, par, outer=True, top=True):
                last = node(X, n - 1) if outer else None
                k = ln0 + 3 * NT - 2 if isinstance(n, int) and n == NT else n * 3 + (ln0 - 1)

                def pick(from_):
                    dve.max(out=mx8, in_=from_)

                def strike(from_):
                    dve.match_replace(out=cand, in_to_replace=mx8, in_values=from_, imm_value=LOWEST)
                if top:
                    wait(dve, s_z0, g - 1 + CR)
                if outer:
                    wait(dve, s_tb, n)
                    dve.tensor_tensor(urow, tb[1 - par], node(R_, n - 1), ALU.add)
                if top:
                    pick(keep)
                dve.drain()
                if outer:
                    dve.bn_stats(bn, urow)
                if top:
                    strike(keep)
                dve.drain()
                if outer:
                    dve.bn_aggr(mv, bn)
                if top:
                    pick(cand)
                dve.drain()
                if outer:
                    variance(LN_EPS_INTER)
                if top:
                    strike(cand)
                dve.drain()
                if outer:
                    inverse_deviation(k)
                    dve.drain()
                if outer:
                    dve.tensor_scalar(urow, urow, mv[:, 0:1], rs, ALU.subtract, ALU.mult)
                if top:
                    pick(cand)
                dve.drain()
                if outer:
                    dve.tensor_tensor(urow, urow, late["s_out"], ALU.mult)
                if top:
                    strike(cand)
                dve.drain()
                if outer:
                    dve.tensor_tensor(urow, urow, late["b_out"], ALU.add)
                if top:
                    pick(cand)
                dve.drain()
                if outer:
                    dve.tensor_tensor(last, last, urow, ALU.add)
                if top:
                    strike(cand)
                dve.drain()
                if outer:
                    dve.bn_stats(bn, last)
                if top:
                    dve.scalar_tensor_tensor(out=top_row, in0=cand, scalar=LOWEST, in1=keep, op0=ALU.is_equal,
                                             op1=ALU.mult)
                dve.drain()
                if outer:
                    dve.bn_aggr(mv, bn)
                if top:
                    dve.tensor_copy(span(ZH[0], (n - 2) * ZW, D), top_row)
                dve.drain()
                if outer:
                    variance(LN_EPS)
                if top:
                    dve.tensor_tensor(span(ZH[0], (n - 2) * ZW + D, D), top_row, span(ZH[0], (n - 2) * ZW, D),
                                      ALU.subtract).then_inc(s_zD, 1)
                dve.drain()
                if outer:
                    inverse_deviation(k + 1)
                    dve.drain()
                    hrow_free(g - 1)
                    dve.tensor_scalar(hrow[1 - par], last, mv[:, 0:1], rs, ALU.subtract, ALU.mult).then_inc(s_row, 1)

            def inter(n, g, par):
                inner(n, g, par)
                outer_and_top(n, g, par)
            inner(0, g0, g0 % 2)
            inner(1, g0 + 1, (g0 + 1) % 2)
            outer_and_top(1, g0 + 1, (g0 + 1) % 2, top=False)
            with dve.Fori(0, (NT - 3) // 2) as j:
                for c in range(2):
                    inter(j * 2 + (2 + c), j * 2 + (g0 + 2 + c), (g0 + c) % 2)
            inter(NT - 1, g0 + NT - 1, (g0 + NT - 1) % 2)
            outer_and_top(NT, g0 + NT, (g0 + NT) % 2)
            outer_and_top(NT + 1, g0 + NT + 1, (g0 + NT + 1) % 2, outer=False)

            chain(dve.tensor_scalar(rdeg[:, :], rdeg[:, :], top_back, None, ALU.mult))

            def last(n, g, h, par):
                agg_read(g - NT)
                chain(dve.scalar_tensor_tensor(out=urow, in0=agg[1 - par][:, 0:D], scalar=one(rdeg, n),
                                               in1=node(R_, n), op0=ALU.mult, op1=ALU.add))
                agg_done()
                chain(dve.tensor_tensor(node(X, n), node(X, n), urow, ALU.add).then_inc(s_done, 1))
            tiles(dve, PH_MAXK, last)

        @block.tensor
        def _(pe):
            pe.sem_inc(s_used, RING)
            pe.sem_inc(s_tp, CR + NT)
            pe.sem_inc(s_mm, CR + NT)
            pe.sem_inc(s_agg, CR)
            pe.wait_ge(s_const, 7)
            pe.wait_ge(s_prep, PREP_ROWS)

            def transpose_rows_of(a, from_):
                for c in range(EB):
                    pe.transpose(ps[:, a % 4, c * P:(c + 1) * P], from_[:, c, :], ident[:, :]).then_inc(s_prep_pe, 1)
            for a, from_ in enumerate((part_f[:, 0], part_f[:, 1], part_f[:, 2], rows[:, 2])):
                transpose_rows_of(a, from_)
            for a in range(2):
                for c in range(EB):
                    m = pe.matmul(ps[0:1, 4 + a, c * P:(c + 1) * P], stat[:, a, c:c + 1], ident[:, :],
                                  start=True, stop=True, skip_group_check=True)
                m.then_inc(s_prep_pe, 1)
            for a, from_ in ((4, part_f[:, 8]), (5, part_f[:, 7])):
                pe.wait_ge(s_prep, PREP_ROWS + a - 3)
                transpose_rows_of(a, from_)
            pe.wait_ge(s_prep, PREP_SCAN)
            for k in range(2):
                m = pe.matmul(ps[:, k, 0:ET], ones_row[0:1, :], scan[0:1, k, 0:ET], start=True, stop=True)
            m.then_inc(s_prep_pe, 1)
            pe.wait_ge(s_prep, PREP_STEPS - 1)
            for k, t in enumerate((2, 6)):
                m = pe.matmul(ps[0:1, 2, k * P:(k + 1) * P], tab_f[:, t:t + 1], ident[:, :], start=True, stop=True,
                              skip_group_check=True)
            m.then_inc(s_prep_pe, 1)
            pe.wait_ge(s_prep, PREP_STEPS)

            def clear(bank):
                return pe.matmul(bank[:, 500:501], zeros[:, :], zeros[:, 0:1], start=True, stop=True,
                                 skip_group_check=True)

            pe.wait_ge(s_raw, 16 * (-(-(ET - 1) // -(-(ET - 1) // RLOADS)) + 1))
            start_walk(pe, mybir.EngineType.PE)
            with pe.Fori(0, NT) as c:
                def begin(i):
                    wait(pe, s_taken, c * PER + (i - 1 + CR))
                    wait(pe, s_takenW, c * PER + (i - 1 + CR))
                    clear(cnt_ps[i % 2])
                    clear(wgt_ps[i % 2])

                def add(k, u, t, i):
                    def product(out_, left, right):
                        return pe.matmul(out_, left, right, start=False, stop=True, skip_group_check=True)
                    wait(pe, s_hotD, k + (u + 1))
                    product(cnt_ps[i % 2][:, 0:GW], part_of(u, O_R, P), part_of(u, O_P, GW))
                    wait(pe, s_hotT, k + (u + 1))
                    product(cnt_ps[i % 2][0:G, GW:GW + DE], hot_t[:, u, :], node(raw, t))
                    wait(pe, s_hotA, k + (u + 1))
                    for a in range(3):
                        m = product(wgt_ps[i % 2][:, 0:GW], part_of(u, O_SW + a * P, P), part_of(u, O_Q, GW))
                    m.then_inc(s_used, 1)

                def end(i):
                    pe.matmul(cnt_ps[i % 2][:, 501:502], zeros[:, :], zeros[:, 0:1], start=False, stop=True,
                              skip_group_check=True).then_inc(s_built, 1)
                walk(pe, mybir.EngineType.PE, c, add, before=begin, after=end)
            pe.wait_ge(s_taken, NG + CR)
            pe.wait_ge(s_takenW, NG + CR)

            def transpose_rows(g, par):
                wait(pe, s_row, g + 1)
                wait(pe, s_hT, g - 1 + CR)
                for k in range(2):
                    m = pe.transpose(tp[par][:, k * P:(k + 1) * P], hrow[par][:, k * P:(k + 1) * P], ident[:, :])
                m.then_inc(s_tp, 1)

            def multiply(g, par, W):
                wait(pe, s_hT, g + 1 + CR)
                wait(pe, s_z0, g - 1 + CR)
                wait(pe, s_zD, g - 1 + CR)
                width = W.shape[2]
                for k in range(2):
                    m = pe.matmul(mmo[par][:, 0:width], hT[par][:, k * P:(k + 1) * P], W[:, k, :],
                                  start=(k == 0), stop=(k == 1))
                m.then_inc(s_mm, 1)

            pe.wait_ge(s_w, 16 * 16)

            def aggregate(i, n, q, h, par, b0, b1):
                if b0 == 0:
                    wait(pe, s_blk[par], h * 16 + 16)
                    wait(pe, s_aggfree, q - 1 + CR)
                for b in range(b0, b1):
                    if i == 2:
                        m = pe.matmul(agg[par][:, 0:D], BLK32[par][:, b * P:(b + 1) * P],
                                      ZFULL[0][:, b * D:(b + 1) * D], start=(b == 0), stop=(b == NT - 1),
                                      skip_group_check=True)
                        continue
                    for part, wide in ((1, D + (i == 0)), (0, D)):
                        m = pe.matmul(agg[par][:, 0:wide], BLK16[par][:, b * P:(b + 1) * P],
                                      ZH[zin(i)][:, b * ZW + part * D:b * ZW + part * D + wide],
                                      start=(b == 0 and part == 1), stop=(b == NT - 1 and part == 0),
                                      skip_group_check=True)
                if b1 == NT:
                    m.then_inc(s_agg, 1)

            def z_ready(phase):
                for s in (s_z0, s_zD):
                    pe.wait_ge(s, NT * (phase + 1) + CR)

            def row_layer(i, W, c0, c1):
                phase = i + 1
                z_ready(i)
                q0, g0 = NT * i, NT * phase
                aggregate(i, 0, q0, q0 // 2, q0 % 2, 0, NT)

                def body(n, q, h, par):
                    aggregate(i, n, q, h, par, 0, c0)
                    transpose_rows(q + (NT - 1), par)
                    aggregate(i, n, q, h, par, c0, c1)
                    multiply(q + (NT - 1), par, W)
                    aggregate(i, n, q, h, par, c1, NT)
                tiles(pe, i, body, first=1)
                g = g0 + NT - 1
                transpose_rows(g, g % 2)
                multiply(g, g % 2, W)

            def conv_transpose(n):
                wait(pe, s_mo, n + 1)
                wait(pe, s_moC, n)
                for k in range(4):
                    m = pe.transpose(conv_t[:, k * P:(k + 1) * P], mean_own[:, k * P:(k + 1) * P], ident[:, :])
                m.then_inc(s_moT, 1)

            def conv_multiply(n):
                wait(pe, s_moC, n + 1)
                wait(pe, s_row, n + NT)
                for k in range(4):
                    m = pe.matmul(conv_ps, mean_ownT[:, k * P:(k + 1) * P],
                                  W_early[:, 0, k % 2, k // 2 * D:(k // 2 + 1) * D], start=(k == 0), stop=(k == 3))
                m.then_inc(s_conv, 1)

            def sage1(n, g, par, half, at0, at1, at2):
                cuts = [0, 9, 14, 17, 21, NT]
                steps = [lambda: conv_transpose(n - 1) if at1 else None,
                         lambda: conv_multiply(n - 1) if at1 else None,
                         lambda: transpose_rows(g - 2, par) if at2 else None,
                         lambda: multiply(g - 2, par, W_early[:, 1]) if at2 else None,
                         lambda: None]
                for k, step in enumerate(steps):
                    if at0:
                        aggregate(0, n, n, half, 1 - par, cuts[k], cuts[k + 1])
                    step()
            def spread_largest(steps, k, cols):
                pe.wait_ge(s_scale, steps)
                for j, c in enumerate(cols):
                    m = pe.matmul(ps[0:1, 7, j * P:(j + 1) * P], scale_f[:, k, c:c + 1], ident[:, :],
                                  start=True, stop=True, skip_group_check=True)
                m.then_inc(s_scale_pe, 1)
                pe.wait_ge(s_scale, steps + 1)
                pe.matmul(ps[:, 7, 2 * P:2 * P + len(cols)], ones_row[0:1, :], scale_f[0:1, k, 10:10 + len(cols)],
                          start=True, stop=True, skip_group_check=True).then_inc(s_scale_pe, 1)

            spread_largest(8, 0, (4, 5))
            z_ready(0)
            pe.wait_ge(s_z2, NT)
            pe.wait_ge(s_ones, 1)
            staggered(pe, PH_SAGE1, sage1)
            pe.wait_ge(s_wlate, 16 * 11)
            row_layer(1, wk(late["W_gcn"], D), 19, 23)
            spread_largest(SCALE_CONV + 4, 1, (4,))
            spread_largest(SCALE_CONV + 14, 2, (4,))
            row_layer(2, wk(late["W_msg"], D), 12, 18)

            i = 3
            z_ready(i)
            q0, g0 = NT * i, NT * PH_INTER
            maxk_w = wk(late["W_maxk"], 2 * D)

            def edges_in(n):
                wait(pe, s_ean, n * 16 + 16)
                pe.transpose(mlp_ps[:, 0:P], ea_now[:, :], ident[:, :]).then_inc(s_eat, 1)

            def edges_add(n, par):
                wait(pe, s_eac, n + 1)
                pe.matmul(agg[par][:, 0:D], eaT[:, :], late["W_edge"][0:DE, :], start=False, stop=False,
                          skip_group_check=True)

            def inner_transpose(n):
                wait(pe, s_inner, n + 1)
                for k in range(2):
                    m = pe.transpose(tv[:, k * P:(k + 1) * P], inner_row[:, k * P:(k + 1) * P], ident[:, :])
                m.then_inc(s_tv, 1)

            def mlp_layer(n, l):
                if l == 0:
                    wait(pe, s_g0, n + 1)
                else:
                    wait(pe, s_g, n * 3 + l)
                W = wk(late[f"mlp{l}"], D)
                for o in range(2):
                    for k in range(2):
                        m = pe.matmul(mlp_ps[:, o * P:(o + 1) * P], W[:, k, o * P:(o + 1) * P],
                                      GT[:, l % 2, k * P:(k + 1) * P], start=(k == 0), stop=(k == 1))
                m.then_inc(s_q, 1)

            def back(n, par):
                wait(pe, s_g, n * 3 + 3)
                for k in range(2):
                    m = pe.transpose(tb[par][:, k * P:(k + 1) * P], GT[:, 1, k * P:(k + 1) * P], ident[:, :])
                m.then_inc(s_tb, 1)

            def inter(n, q, h, par, here=True, back1=True, back2=True):
                cuts = [0, 2, 6, 9, 15, 21, NT, NT, NT]
                steps = [lambda: edges_in(n) if here else None,
                         lambda: (edges_add(n, par) if here else None,
                                  inner_transpose(n - 1) if back1 else None),
                         lambda: mlp_layer(n - 1, 0) if back1 else None,
                         lambda: mlp_layer(n - 1, 1) if back1 else None,
                         lambda: mlp_layer(n - 1, 2) if back1 else None,
                         lambda: transpose_rows(q + (NT - 2), 1 - par) if back2 else None,
                         lambda: back(n - 1, par) if back1 else None,
                         lambda: multiply(q + (NT - 2), 1 - par, maxk_w) if back2 else None]
                for s, f in enumerate(steps):
                    if here and cuts[s] < cuts[s + 1]:
                        aggregate(i, n, q, h, par, cuts[s], cuts[s + 1])
                    f()

            inter(0, q0, q0 // 2, q0 % 2, back1=False, back2=False)
            inter(1, q0 + 1, (q0 + 1) // 2, (q0 + 1) % 2, back2=False)
            with pe.Fori(0, (NT - 3) // 2) as j:
                for c in range(2):
                    inter(j * 2 + (2 + c), j * 2 + (q0 + 2 + c), j + (q0 + 2 + c) // 2, (q0 + c) % 2)
            q = q0 + NT - 1
            inter(NT - 1, q, q // 2, q % 2)
            inter(NT, q + 1, None, (q + 1) % 2, here=False)
            inter(NT + 1, q + 2, None, (q + 2) % 2, here=False, back1=False)

            z_ready(4)
            tiles(pe, 4, lambda n, q, h, par: aggregate(4, n, q, h, par, 0, NT))


_WEIGHTS = ["L0_gnn_W_l1", "L0_gnn_b1", "L0_gnn_W_r1", "L0_gnn_W_l2", "L0_gnn_b2", "L0_gnn_W_r2", "L1_gnn_W",
            "L1_gnn_b", "L2_gnn_W_message", "L2_gnn_mlp_W0", "L2_gnn_mlp_b0", "L2_gnn_mlp_W1", "L2_gnn_mlp_b1",
            "L2_gnn_mlp_W2", "L2_gnn_mlp_b2", "L2_gnn_ln_aggr_scale", "L2_gnn_ln_aggr_bias", "L2_gnn_ln_out_scale",
            "L2_gnn_ln_out_bias", "L3_gnn_W_self", "L3_gnn_W_neigh"]
_INPUTS = ["x", "src", "dst", "edge_attr_64", "edge_weight"] + _WEIGHTS


def kernel(**inputs):
    import concourse.bacc as bacc
    from concourse.bass_utils import run_bass_kernel_spmd as run

    nc = bacc.Bacc("TRN2", target_bir_lowering=False, num_devices=1)
    arrays, aps = {}, {}
    for name in _INPUTS:
        arrays["in_" + name] = np.ascontiguousarray(inputs[name])
        a = arrays["in_" + name]
        aps[name] = nc.dram_tensor("in_" + name, a.shape, mybir.dt.from_np(a.dtype), kind="ExternalInput").ap()
    out = nc.dram_tensor("out_0", (N, D), F32, kind="ExternalOutput").ap()
    build(nc, aps["x"], aps["src"], aps["dst"], aps["edge_attr_64"], aps["edge_weight"],
          {k: aps[k] for k in _WEIGHTS}, out)
    return run(nc, [arrays], core_ids=[0]).results[0]["out_0"]
```
